# Optimizing a Trainium2 kernel written in Bass

```python
import numpy as np
import jax
import jax.numpy as jnp

def _softmax(x, axis=-1):
    return jax.nn.softmax(x, axis=axis)

def _gelu(x):
    return jax.nn.gelu(x, approximate=True)

def _silu(x):
    return jax.nn.silu(x)

def _sigmoid(x):
    return jax.nn.sigmoid(x)

def _layernorm(x, axis=-1, eps=1e-05):
    m = jnp.mean(x, axis=axis, keepdims=True)
    v = jnp.var(x, axis=axis, keepdims=True)
    return (x - m) / jnp.sqrt(v + eps)

def _scatter_add(tgt, idx, src, axis=0):
    return tgt.at[idx].add(src)

def _segment_sum(src, seg, n):
    return jax.ops.segment_sum(src, seg, n)
kernel_name = 'mk_hybrid_d1_jaxref_r8_706317'

def setup_inputs(seed: int=0):
    np.random.seed(seed)
    _w = jnp.asarray

    def _L0_attn_a_setup():
        import jax, jax.numpy as jnp
        import numpy as np
        H = 16
        SB_RATIO = 0.1
        RB_RATIO = 0.5
        ROPE_BASE = 10000.0

        def _rotate_half(x):
            hd = x.shape[-1]
            x1, x2 = (x[..., :hd // 2], x[..., hd // 2:])
            return jnp.concatenate([-x2, x1], axis=-1)
        key = jax.random.key(seed)
        ks = jax.random.split(key, 6)
        B, T, D = (1, 256, 256)
        s = 0.02
        return {'hidden_states': jax.random.normal(ks[0], (B, T, D), jnp.float32), 'wq': jax.random.normal(ks[1], (D, D), jnp.float32) * s, 'wk': jax.random.normal(ks[2], (D, D), jnp.float32) * s, 'wv': jax.random.normal(ks[3], (D, D), jnp.float32) * s, 'wo': jax.random.normal(ks[4], (D, D), jnp.float32) * s, 'bern_u': jax.random.uniform(ks[5], (B, H), jnp.float32)}
    _L0_attn_a_in = _L0_attn_a_setup()

    def _L0_attn_b_setup():
        import jax, jax.numpy as jnp
        import numpy as np
        B, S, E, H = (2, 256, 256, 16)
        NOPE, ROPE, VD = (128, 64, 128)
        QH = NOPE + ROPE
        LORA = 64
        ROPE_THETA = 10000.0
        EPS = 1e-06

        def _rope(xp, cos, sin):
            d2 = xp.shape[-1] // 2
            x1, x2 = (xp[..., :d2], xp[..., d2:])
            return jnp.concatenate([x1 * cos - x2 * sin, x2 * cos + x1 * sin], axis=-1)
        key = jax.random.key(seed)
        ks = jax.random.split(key, 5)
        sd = lambda n: 1.0 / np.sqrt(n)
        return {'x': jax.random.normal(ks[0], (B, S, E), jnp.float32), 'wq': jax.random.normal(ks[1], (E, H * QH), jnp.float32) * sd(E), 'wkv_a': jax.random.normal(ks[2], (E, LORA + ROPE), jnp.float32) * sd(E), 'wkv_b': jax.random.normal(ks[3], (LORA, H * (NOPE + VD)), jnp.float32) * sd(LORA), 'wo': jax.random.normal(ks[4], (H * VD, E), jnp.float32) * sd(H * VD), 'kv_norm_scale': jnp.ones((LORA,), jnp.float32)}
    _L0_attn_b_in = _L0_attn_b_setup()

    def _L0_ffn_setup():
        import jax, jax.numpy as jnp
        import numpy as np
        import math
        N_EMBD = 256
        N_HEAD = 16
        HEAD_DIM = N_EMBD // N_HEAD
        B, T = (2, 256)
        key = jax.random.key(seed)
        k1, k2, k3 = jax.random.split(key, 3)
        x = jax.random.normal(k1, (B, T, N_EMBD), dtype=jnp.float32)
        W_gate = jax.random.normal(k2, (N_HEAD, N_EMBD), dtype=jnp.float32) * 0.02
        W_qkv = jax.random.normal(k3, (3 * N_EMBD, N_EMBD), dtype=jnp.float32) * 0.02
        return {'x': x, 'W_gate': W_gate, 'W_qkv': W_qkv}
    _L0_ffn_in = _L0_ffn_setup()
    _d = {'L0_attn_a_hidden_states': _L0_attn_a_in['hidden_states'], 'L0_attn_a_wq': _L0_attn_a_in['wq'], 'L0_attn_a_wk': _L0_attn_a_in['wk'], 'L0_attn_a_wv': _L0_attn_a_in['wv'], 'L0_attn_a_wo': _L0_attn_a_in['wo'], 'L0_attn_a_bern_u': _L0_attn_a_in['bern_u'], 'L0_attn_b_wq': _L0_attn_b_in['wq'], 'L0_attn_b_wkv_a': _L0_attn_b_in['wkv_a'], 'L0_attn_b_wkv_b': _L0_attn_b_in['wkv_b'], 'L0_attn_b_wo': _L0_attn_b_in['wo'], 'L0_attn_b_kv_norm_scale': _L0_attn_b_in['kv_norm_scale'], 'L0_ffn_W_gate': _L0_ffn_in['W_gate'], 'L0_ffn_W_qkv': _L0_ffn_in['W_qkv']}
    _x0 = _d['L0_attn_a_hidden_states']
    _d['L0_attn_a_hidden_states'] = jax.random.normal(jax.random.fold_in(jax.random.key(seed), 1), (8, 256, 256), dtype=_x0.dtype)
    del _x0
    return _d

def reference(L0_attn_a_hidden_states, L0_attn_a_wq, L0_attn_a_wk, L0_attn_a_wv, L0_attn_a_wo, L0_attn_a_bern_u, L0_attn_b_wq, L0_attn_b_wkv_a, L0_attn_b_wkv_b, L0_attn_b_wo, L0_attn_b_kv_norm_scale, L0_ffn_W_gate, L0_ffn_W_qkv):

    def _L0_attn_a_ref(hidden_states, wq, wk, wv, wo, bern_u):
        import jax, jax.numpy as jnp
        import numpy as np
        H = 16
        SB_RATIO = 0.1
        RB_RATIO = 0.5
        ROPE_BASE = 10000.0

        def _rotate_half(x):
            hd = x.shape[-1]
            x1, x2 = (x[..., :hd // 2], x[..., hd // 2:])
            return jnp.concatenate([-x2, x1], axis=-1)
        B, T, D = hidden_states.shape
        hd = D // H
        h = jnp.nan_to_num(hidden_states, nan=0.0, posinf=10000.0, neginf=-10000.0)

        def proj(w):
            return (h @ w.T).reshape(B, T, H, hd).transpose(0, 2, 1, 3)
        Q, K, V = (proj(wq), proj(wk), proj(wv))
        inv_freq = 1.0 / ROPE_BASE ** (jnp.arange(0, hd, 2, dtype=jnp.float32) / hd)
        pos = jnp.arange(T, dtype=jnp.float32)
        freqs = pos[:, None] * inv_freq[None, :]
        emb = jnp.concatenate([freqs, freqs], axis=-1)
        cos, sin = (jnp.cos(emb)[None, None], jnp.sin(emb)[None, None])
        Q = Q * cos + _rotate_half(Q) * sin
        K = K * cos + _rotate_half(K) * sin
        sb = max(0, min(int(SB_RATIO * T), T))
        rb = max(0, min(int(RB_RATIO * T), T - sb))
        kidx = jnp.arange(T)
        cam = (kidx < sb) | (kidx >= T - rb)
        scores = jnp.einsum('bhqd,bhkd->bhqk', Q, K) / np.sqrt(hd).astype(np.float32)
        neg = jnp.finfo(scores.dtype).min
        scores = jnp.where(cam[None, None, None, :], scores, neg)
        scores = jnp.nan_to_num(scores, nan=neg)
        probs = jax.nn.softmax(scores, axis=-1)
        if 0 < rb < T:
            e = T - rb
            ws = e + 1
            if T - ws > 0:
                last = probs[..., -1, :]
                mean_attn = last[..., ws:].mean(axis=-1) + 1e-06
                p = jnp.clip(last[..., e] / mean_attn, 0.0, 1.0)
                p = jnp.nan_to_num(p, nan=0.0, posinf=1.0, neginf=0.0)
                mask = (bern_u < p).astype(V.dtype)
                v_e = V[..., e, :] * mask[..., None] / rb
                end = min(T, ws + rb)
                V = V.at[..., ws:end, :].add(v_e[..., None, :])
        out = jnp.einsum('bhqk,bhkd->bhqd', probs, V)
        out = out.transpose(0, 2, 1, 3).reshape(B, T, D) @ wo.T
        return jnp.nan_to_num(out, nan=0.0, posinf=10000.0, neginf=-10000.0)

    def _L0_attn_b_ref(x, wq, wkv_a, wkv_b, wo, kv_norm_scale):
        import jax, jax.numpy as jnp
        import numpy as np
        B, S, E, H = (2, 256, 256, 16)
        NOPE, ROPE, VD = (128, 64, 128)
        QH = NOPE + ROPE
        LORA = 64
        ROPE_THETA = 10000.0
        EPS = 1e-06

        def _rope(xp, cos, sin):
            d2 = xp.shape[-1] // 2
            x1, x2 = (xp[..., :d2], xp[..., d2:])
            return jnp.concatenate([x1 * cos - x2 * sin, x2 * cos + x1 * sin], axis=-1)
        b, s, _ = x.shape
        q = (x @ wq).reshape(b, s, H, QH).transpose(0, 2, 1, 3)
        q_nope, q_pe = (q[..., :NOPE], q[..., NOPE:])
        kva = x @ wkv_a
        ckv, k_pe = (kva[..., :LORA], kva[..., LORA:])
        ckv = ckv * jax.lax.rsqrt(jnp.mean(ckv * ckv, axis=-1, keepdims=True) + EPS)
        ckv = ckv * kv_norm_scale
        kv = (ckv @ wkv_b).reshape(b, s, H, NOPE + VD).transpose(0, 2, 1, 3)
        k_nope, v = (kv[..., :NOPE], kv[..., NOPE:])
        pos = jnp.arange(s, dtype=jnp.float32)
        inv = 1.0 / ROPE_THETA ** (jnp.arange(0, ROPE, 2, dtype=jnp.float32) / ROPE)
        ang = pos[:, None] * inv
        cos, sin = (jnp.cos(ang), jnp.sin(ang))
        q_pe = _rope(q_pe, cos, sin)
        k_pe = _rope(k_pe[:, None, :, :], cos, sin)
        qs = jnp.concatenate([q_nope, q_pe], axis=-1)
        ks_ = jnp.concatenate([k_nope, jnp.broadcast_to(k_pe, (b, H, s, ROPE))], axis=-1)
        scale = QH ** (-0.5)
        scores = jnp.einsum('bhqd,bhkd->bhqk', qs, ks_) * scale
        causal = jnp.tril(jnp.ones((s, s), dtype=bool))
        scores = jnp.where(causal, scores, jnp.finfo(scores.dtype).min)
        attn = jax.nn.softmax(scores, axis=-1)
        out = jnp.einsum('bhqk,bhkd->bhqd', attn, v)
        out = out.transpose(0, 2, 1, 3).reshape(b, s, H * VD)
        return out @ wo

    def _L0_ffn_ref(x, W_gate, W_qkv):
        import jax, jax.numpy as jnp
        import numpy as np
        import math
        N_EMBD = 256
        N_HEAD = 16
        HEAD_DIM = N_EMBD // N_HEAD
        B, T = (2, 256)
        Bb, Tt, C = x.shape
        H, hd = (N_HEAD, HEAD_DIM)
        gating = jax.nn.softmax(x @ W_gate.T, axis=-1)
        idx = jnp.argmax(gating, axis=-1)
        indicator = jax.nn.one_hot(idx, H, dtype=gating.dtype)
        top1_val = jnp.max(gating, axis=-1, keepdims=True)
        gating_top1 = indicator * top1_val
        qkv = x @ W_qkv.T
        q, k, v = jnp.split(qkv, 3, axis=-1)
        k = k.reshape(Bb, Tt, H, hd)
        v = v.reshape(Bb, Tt, H, hd)
        k_shared = jnp.einsum('bth,bthd->btd', indicator, k)
        v_shared = jnp.einsum('bth,bthd->btd', gating_top1, v)
        q = q.reshape(Bb, Tt, H, hd).transpose(0, 2, 1, 3)
        att = jnp.einsum('bhqd,bkd->bhqk', q, k_shared) * (1.0 / math.sqrt(hd))
        causal = jnp.tril(jnp.ones((Tt, Tt), dtype=bool))
        att = jnp.where(causal[None, None, :, :], att, -jnp.inf)
        att = jax.nn.softmax(att, axis=-1)
        y = jnp.einsum('bhqk,bkd->bhqd', att, v_shared)
        y = y.transpose(0, 2, 1, 3).reshape(Bb, Tt, C)
        return y
    x = L0_attn_a_hidden_states
    x = x + _L0_attn_a_ref(_layernorm(x, axis=-1), L0_attn_a_wq, L0_attn_a_wk, L0_attn_a_wv, L0_attn_a_wo, L0_attn_a_bern_u)
    x = x + _L0_ffn_ref(_layernorm(x, axis=-1), L0_ffn_W_gate, L0_ffn_W_qkv)
    x = x + _L0_attn_b_ref(_layernorm(x, axis=-1), L0_attn_b_wq, L0_attn_b_wkv_a, L0_attn_b_wkv_b, L0_attn_b_wo, L0_attn_b_kv_norm_scale)
    x = x + _L0_ffn_ref(_layernorm(x, axis=-1), L0_ffn_W_gate, L0_ffn_W_qkv)
    return x

_drawn_inputs = setup_inputs


def setup_inputs(seed=0):
    import zlib

    import numpy as np

    out = dict(_drawn_inputs(seed))
    spreads = {'L0_attn_b_kv_norm_scale': (1.0, 0.2)}
    factors = {'L0_attn_a_wq': 8.0,
     'L0_attn_a_wk': 8.0,
     'L0_attn_a_wv': 4.821,
     'L0_attn_a_wo': 4.958,
     'L0_attn_a_bern_u': 8.0,
     'L0_ffn_W_gate': 7.907,
     'L0_ffn_W_qkv': 6.805}
    for name, (base, spread) in spreads.items():
        noise = np.random.default_rng([zlib.crc32(name.encode()), seed]).standard_normal(out[name].shape)
        drawn = base * np.exp(spread * noise) if base else spread * noise
        out[name] = jnp.asarray(drawn.astype(out[name].dtype))
    for name, factor in factors.items():
        out[name] = (out[name] * factor).astype(out[name].dtype)
    return out
```

```python
from contextlib import ExitStack

import concourse.bass as bass
from concourse import mybir

B, T, D, H = 8, 256, 256, 16
P = 128
NT = T // P
NC = D // P
HD = D // H
NOPE, ROPE, VD, LORA = 128, 64, 128, 64
QH = NOPE + ROPE
SB, RB = T // 10, T // 2
E_TOK = T - RB
KA = SB + RB
KA_PAD = RB + 64
G = 4
VC = 32
STK = 96
ARENA = 12544
N_FILLS, N_DVE_FILLS = 7, 6
N_ARENA = 15
FLT_MAX = 3.4028234663852886e38
BIG = 1.0e4
EPS_LN, EPS_RMS = 1e-5, 1e-6
SCALE_B = QH ** -0.5
C_ID, C_MASK = 0, P
C_COS, C_SIN, C_COSK, C_SINK = 256, 512, 768, 1024
C_HM = 1280
C_DESC = C_HM + NC * H
C_COSB = C_DESC + H
C_SINB = C_COSB + NT * ROPE
C_END = C_SINB + NT * ROPE
F_V, F_KG = D, 2 * D
F_COLS = 3 * D + H
A_COLS = 5 * D
W_KVA = NOPE
W_ABS = LORA + ROPE
W_PE = W_ABS + H * LORA
W_COLS = W_PE + H * ROPE


Q_SLOTS = {4: (0, 1), 5: (2,), 6: (3, 4), 7: (5,), 8: (6, 7)}
QT_SLOTS = {10: (0, 1), 11: (2,), 12: (3, 4), 13: (5,), 14: (6,), 15: (7,)}


def slot_of(h):
    return 1 if h == H - 1 else h % 3


def before(h):
    for back in range(h - 1, h - H - 1, -1):
        if slot_of(back % H) == slot_of(h):
            return back + 1


def hybrid_layers_kernel(nc, x_in, a_wT, a_woT, a_u, f_wT, b_wqn, b_wqp, b_wkT, b_wvT, b_wo, b_wkva,
                         b_norm, consts, consts16, out):
    f32, f32r, bf16, i32 = mybir.dt.float32, mybir.dt.float32r, mybir.dt.bfloat16, mybir.dt.int32
    ALU = mybir.AluOpType
    ACT = mybir.ActivationFunctionType
    AX = mybir.AxisListType
    ds = bass.ds

    ctx = ExitStack()
    with ctx:
        def sb(name, shape, dt=f32, stack=ctx):
            return stack.enter_context(nc.sbuf_tensor(name, shape, dt))

        def sem(name):
            return ctx.enter_context(nc.semaphore(name))

        def signals(layer, names):
            return SimpleNamespace(**{n: sem(f"{layer}_{n}") for n in names.split()})

        x_all = sb("x_all", [P, B * NT * D])
        cst = sb("cst", [P, C_END])
        cst16 = sb("cst16", [H, D + P + 1])
        ident_bf = sb("ident_bf", [P, P], bf16)
        mask_bf = sb("mask_bf", [P, P], bf16)
        big_pos = sb("big_pos", [P, 1])
        big_neg = sb("big_neg", [P, 1])
        expo = sb("expo", [P, NT])
        stats = sb("stats", [P, NT, 6])
        mv = sb("mv", [P, NT, 2])
        var_eps = sb("var_eps", [P, NT])
        rstd = sb("rstd", [P, NT])
        xn = sb("xn", [P, NT, D])
        hT = sb("hT", [P, NC, T])
        x_hi = sb("x_hi", [P, NC, T], f32r)
        x_lo = sb("x_lo", [P, NC, T], f32r)
        f_hi = sb("f_hi", [P, NC, F_COLS], f32r)
        f_lo = sb("f_lo", [P, NC, F_COLS], f32r)
        q_hi = sb("q_hi", [P, NC, T], f32r)
        q_lo = sb("q_lo", [P, NC, T], f32r)
        q_stack = [sb(f"q_stack{i}", [STK, H, T], f32r) for i in range(2)]
        kf_stack = [sb(f"kf_stack{i}", [STK, T], f32r) for i in range(2)]
        v_sh = [sb(f"v_sh{i}", [P, NT, VC]) for i in range(2)]
        neg_max = sb("neg_max", [P, 4, NT])
        sums = sb("sums", [P, 4, NT])
        inv_sum = sb("inv_sum", [P, 4, NT])
        probs = sb("probs", [P, 4, 3 * P])
        probsT = sb("probsT", [P, 8, 3 * P])
        oT = sb("oT", [P, 2, T])
        recip = sb("recip", [P, 2, NT, G])
        y = sb("y", [P, NT, D])
        k48 = sb("k48", [P, NT, 3 * HD], f32r)
        norm_bc = sb("norm_bc", [P, LORA])
        sq_sum = sb("sq_sum", [P, NT])
        rms = sb("rms", [P, NT])
        arena = sb("arena", [P, ARENA])

        ident = cst[:, C_ID:C_ID + P]
        ps = [ctx.enter_context(nc.psum_tensor(f"bank{i}", [P, 512], f32)) for i in range(8)]
        ps_s, ps_t, ps_o, ps_a, ps_b = ps[0:3], ps[3:5], ps[5], ps[6], ps[7]

        scr_q = [nc.dram_tensor(f"scr_q{i}", [D, T], f32, kind="Internal").ap() for i in range(2)]
        scr_k = [nc.dram_tensor(f"scr_k{i}", [D, T], f32, kind="Internal").ap() for i in range(2)]


        s_const = sem("constants_loaded")
        s_x = sem("x_loaded")
        s_w = sem("small_weights_loaded")
        s_fill = sem("pool_fills_done")
        s_dfill = sem("dve_fills_done")
        s_arena = sem("arena_initialised")
        s_split = sem("small_weights_split")
        s_stage = sem("attn_b_weights_staged")
        s_out = sem("out_stored")
        q_put = [sem(f"q_put{i}") for i in range(3)]
        q_got = [sem(f"q_got{i}") for i in range(3)]
        k_put, k_got = sem("k_put"), sem("k_got")
        b_prep, b_hi, b_lo, b_mvo = sem("b_prep"), sem("b_hi"), sem("b_lo"), sem("b_mvo")

        ON_ACT = {"a": (3, 7, 11, 15), "f": (3, 7, 11, 15), "b": tuple(range(H))}

        def signals(layer, kind, **own):
            n_act = len(ON_ACT[kind])
            per = dict(stats=4, rstd=2, xn=1, xT=1, x_hi=1, x_lo=1, scores=H, maxed=H, exp=H, pT_ps=H,
                       copy_dve=H - n_act, copy_act=n_act, oT=2 * H // G if kind == "b" else H // G,
                       o_ps=2 * H // G if kind == "b" else H // G, x_done=1, **own)
            return dict(kind=kind, per=per, past=0, **{n: sem(f"{layer}_{n}") for n in per})

        HEADS16 = dict(r_ps=H // G, y=3 * H // G, q_hi=1, q_lo=1)
        sa = signals("attn_a", "a", **HEADS16, hT=2, q_ps=1, qr_ps=1, q_rot1=1, q_rot2=1, q_f=1, k_ps=1, kr_ps=1,
                     k_rot1=1, k_rot2=1, k_f=1, k_hi=1, k_lo=1, q_last=2, e_ps=1, e_dve=13, e_exp=3, v_ps=1,
                     v_big=1, v_small=1, small_in=H // G, small_ps=H // G, rep=2, small=H // G, yT_ps=1, yT=1, wo_ps=1, guarded=6)
        sf = [signals("ffn", "f", **HEADS16, q_ps=1, kg0_ps=1, kg1_ps=1, v_ps=1, gate=11, gate_exp=1, k_sel=3,
                      k48=3, kT_ps=1, k_stack=1, v_sel=2)]
        sf.append({**sf[0], "past": B})
        sm = signals("attn_b", "b", kva_ps=1, kva=3, rms=2, k_tok=2, kT_ps=1, kT=1, qa_ps=4, qa_out=4, qr_ps=4,
                     qr_dve=4, qr_out=4, qT_ps=8, qT_act=4, qT_dve=4, normed=2 * H, wo_ps=H // 2)

        def at(s, name, b, n):
            per = s["per"][name]
            return s[name], b * per + ((s["past"] + 1) * per + n)

        def wait_apart(eng, signal, value):
            value = value if isinstance(value, int) else eng.to_reg(value)
            eng.wait_ge(s_const, 48)
            eng.wait_ge(signal, value)

        def copied(s, b, h, act):
            if h < 0:
                b, h = b - 1, h + H
            return at(s, "copy_act" if act else "copy_dve", b,
                      sum((k in ON_ACT[s["kind"]]) == act for k in range(h + 1)))

        def on_act(s, h):
            return h % H in ON_ACT[s["kind"]]

        def x_tile(b, t):
            return x_all[:, ds(b * (NT * D) + t * D, D)]

        def x_batch(b):
            return x_all[:, ds(b * (NT * D), NT * D)]

        def halves(p):
            return p[:, :].rearrange("p (t d) -> p t d", t=2)

        scope_a, scope_b = ExitStack(), ExitStack()
        a_hi = sb("a_hi", [P, NC, A_COLS], f32r, scope_a)
        a_lo = sb("a_lo", [P, NC, A_COLS], f32r, scope_a)
        wo_a = sb("wo_a", [P, NC, D], f32, scope_a)
        ka_stack = [sb(f"ka_stack{i}", [STK, H, KA_PAD], f32r, scope_a) for i in range(2)]
        k_hi = sb("k_hi", [P, NC, T], f32r, scope_a)
        k_lo = sb("k_lo", [P, NC, T], f32r, scope_a)
        rep_hi = sb("rep_hi", [P, NC, P], f32r, scope_a)
        rep_lo = sb("rep_lo", [P, NC, P], f32r, scope_a)
        scope_a.close()
        wb_hi = sb("wb_hi", [P, NC, W_COLS], f32r, scope_b)
        wb_lo = sb("wb_lo", [P, NC, W_COLS], f32r, scope_b)
        m_vo = sb("m_vo", [P, H // 2, D], f32, scope_b)
        kva_tok = sb("kva_tok", [P, NT, W_ABS], f32, scope_b)
        kv_tok = [sb(f"kv_tok{i}", [P, NT, W_ABS], f32, scope_b) for i in range(2)]
        kbT = [sb(f"kbT{i}", [P, T], f32, scope_b) for i in range(2)]
        k_rot = sb("k_rot", [P, 2, NT, ROPE], f32, scope_b)
        scope_b.close()

        def cut(*shapes):
            lo, views = 0, []
            for shape in shapes:
                n = 1
                for k in shape:
                    n *= k
                v, names = arena[:, lo:lo + n], "abcd"[:len(shape)]
                if len(shape) > 1:
                    v = v.rearrange(f"p ({' '.join(names)}) -> p {' '.join(names)}",
                                    **{k: m for k, m in zip(names[1:], shape[1:])})
                views.append(v)
                lo += n
            assert lo <= ARENA
            return views

        st_a, st_f = cut((NC, A_COLS), (NC, F_COLS))
        (pg, s_guard, rot1, rot2, krot1, krot2, q_f, k_f, v_big0, v_big1, v_blk0, v_blk1, psmT, e_row, e_s, q_bd,
         b_row, yT, guard_t, guard_z, inf_m, psm) = cut(
            (2, NT, G, 160), (2, NT, 160), (NC, T), (NC, T), (NC, T), (NC, T), (NC, T), (NC, T), (H, VC), (H, VC),
            (G, G, VC), (G, G, VC), (2, T), (KA,), (16,), (NC, H), (D,), (NC, T), (NT * D,), (NT * D,), (NT * D,),
            (2, NT, P))
        v_big, v_blk = [v_big0, v_big1], [v_blk0, v_blk1]
        lg, g_s, g_d, g_e, g_eq, g_hot, g_hotv, g_pick, kv_sh = cut(
            (NT, H), (NT, 4), (NT, H), (NT, H), (NT, H), (NT, H), (NT, H), (NT, D), (NT, HD))
        st_wqn, st_wo, st_wk, st_wv, st_pe = cut((H, D), (H, D), (H, LORA), (H, LORA), (NC, W_ABS + H * ROPE))
        qT0, qT1, q_tok = cut((H, T), (H, T), (NT, H, P))
        qT = [qT0, qT1]
        rope1, rope2 = hT, y

        X, AW, FW, WB = (x_hi, x_lo), (a_hi, a_lo), (f_hi, f_lo), (wb_hi, wb_lo)

        def cols(pair, lo, n):
            return tuple((lambda c, w=w: w[:, c, lo:lo + n]) for w in pair)

        def mm3(out_ap, lhs, rhs, stop=True):
            (lh, ll), (rh, rl) = lhs, rhs
            steps = [(l, r, c) for c in range(NC) for l, r in ((lh, rh), (lh, rl), (ll, rh))]
            for i, (l, r, c) in enumerate(steps):
                last = nc.tensor.matmul(out_ap, l(c), r(c), start=i == 0, stop=stop and i == len(steps) - 1)
            return last

        def run_batches(eng, first, body):
            first()
            with eng.Fori(0, B - 2, 2) as b:
                body(b, 0, False)
                body(b + 1, 1, False)
            body(B - 2, 0, False)
            body(B - 1, 1, True)

        def dve_stats(s, b):
            v = nc.vector
            for t in range(NT):
                v.bn_stats(stats[:, t, :], x_tile(b, t)).then_inc(s["stats"], 1)
            wait_apart(v, *at(s, "stats", b, 2))
            for t in range(NT):
                v.bn_aggr(mv[:, t, :], stats[:, t, :]).then_inc(s["stats"], 1)

        def pool_rstd(s, b):
            g = nc.gpsimd
            wait_apart(g, *at(s, "stats", b, 4))
            g.tensor_scalar(var_eps[:, :], mv[:, :, 1], EPS_LN, None, ALU.add).then_inc(s["rstd"], 1)
            g.wait_ge(*at(s, "rstd", b, 1))
            g.tensor_tensor(rstd[:, :], var_eps[:, :], expo[:, :], ALU.pow).then_inc(s["rstd"], 1)

        def dve_normalize(s, b):
            v = nc.vector
            v.wait_ge(*at(s, "rstd", b, 2))
            v.wait_ge(*at(s, "xT", b, 0))
            for t in range(NT):
                last = v.tensor_scalar(xn[:, t, :], x_tile(b, t), mv[:, t, 0:1], rstd[:, t:t + 1],
                                       ALU.subtract, ALU.mult)
            last.then_inc(s["xn"], 1)

        def pe_transpose_x(s, b):
            nc.tensor.wait_ge(*at(s, "xn", b, 1))
            for c in range(NC):
                for t in range(NT):
                    last = nc.tensor.transpose(halves(ps_a)[:, c, t * P:(t + 1) * P], xn[:, t, c * P:(c + 1) * P],
                                               ident)
            last.then_inc(s["xT"], 1)

        def act_x_hi(s, b):
            nc.scalar.wait_ge(*at(s, "xT", b, 1))
            nc.scalar.activation(x_hi[:, :, :], halves(ps_a), ACT.Copy).then_inc(s["x_hi"], 1)

        def dve_x_lo(s, b):
            nc.vector.wait_ge(*at(s, "x_hi", b, 1))
            nc.vector.tensor_tensor(x_lo[:, :, :], halves(ps_a), x_hi[:, :, :].bitcast(f32),
                                    ALU.subtract).then_inc(s["x_lo"], 1)

        def pe_transpose_probs(s, b, h, blocks):
            pe = nc.tensor
            pe.wait_ge(*copied(s, b, h - 2, on_act(s, h - 2)))
            for i, block in enumerate(blocks):
                last = pe.transpose(ps_t[h % 2][:, i * P:(i + 1) * P], block, ident)
            last.then_inc(s["pT_ps"], 1)

        def copy_probs(eng, s, b, h, n, group):
            act = on_act(s, h)
            eng.wait_ge(*at(s, "pT_ps", b, h + 1))
            eng.wait_ge(*at(s, "o_ps", b, h // group + 1 - 8 // group))
            if act:
                nc.scalar.activation(probsT[:, h % 8, 0:n], ps_t[h % 2][:, 0:n], ACT.Copy).then_inc(s["copy_act"], 1)
            else:
                nc.vector.tensor_copy(probsT[:, h % 8, 0:n], ps_t[h % 2][:, 0:n]).then_inc(s["copy_dve"], 1)

        def pe_wait_copies(s, b, h0, n):
            for act in (True, False):
                mine = [h for h in range(h0, h0 + n) if on_act(s, h) == act]
                if mine:
                    nc.tensor.wait_ge(*copied(s, b, mine[-1], act))

        def pe_untranspose(s, b, g):
            pe = nc.tensor
            pe.wait_ge(*at(s, "oT", b, g + 1))
            pe.wait_ge(*at(s, "y", b, 3 * g))
            for t in range(NT):
                last = pe.transpose(ps_o[:, T + t * P:T + (t + 1) * P], oT[:, g % 2, t * P:(t + 1) * P], ident)
            last.then_inc(s["r_ps"], 1)

        def act_oT(s, b, g):
            act = nc.scalar
            act.wait_ge(*at(s, "o_ps", b, g + 1))
            act.wait_ge(*at(s, "r_ps", b, g - 1))
            act.activation(oT[:, g % 2, :], ps_o[:, 0:T], ACT.Copy).then_inc(s["oT"], 1)

        def dve_divide(s, b, g):
            v = nc.vector
            v.wait_ge(*at(s, "r_ps", b, g + 1))
            r = ps_o[:, T:2 * T].rearrange("p (t g c) -> p t g c", t=NT, g=G)
            v.reciprocal(recip[:, g % 2], r[:, :, :, HD]).then_inc(s["y"], 1)
            v.wait_ge(*at(s, "y", b, 3 * g + 1))
            yv = y[:, :, g * G * HD:(g + 1) * G * HD].rearrange("p t (g d) -> p t g d", g=G)
            for t in range(NT):
                v.tensor_tensor(yv[:, t], r[:, t, :, 0:HD],
                                recip[:, g % 2, t, :].unsqueeze(2).to_broadcast([P, G, HD]),
                                ALU.mult).then_inc(s["y"], 1)

        blk = ctx.enter_context(nc.Block())

        @blk.sync
        def _(sp):
            sp.dma_start(x_all[:, 0:NT * D].rearrange("p (t d) -> p t d", t=NT),
                         x_in[0].rearrange("(t p) d -> p t d", p=P)).then_inc(s_x, 16)
            sp.dma_start(cst[:, :], consts).then_inc(s_const, 16)
            sp.dma_start(cst16[:, 0:D + P], consts16).then_inc(s_const, 16)
            sp.dma_start(cst16[:, D + P:D + P + 1], a_u).then_inc(s_const, 16)
            sp.dma_start(st_a, a_wT.rearrange("(c p) n -> p c n", p=P)).then_inc(s_w, 16)
            sp.dma_start(st_f, f_wT.rearrange("(c p) n -> p c n", p=P)).then_inc(s_w, 16)
            sp.dma_start(wo_a[:, :, :], a_woT.rearrange("(c p) n -> p c n", p=P)).then_inc(s_w, 16)
            sp.dma_start(norm_bc[:, :], b_norm.partition_broadcast(P)).then_inc(s_w, 16)
            for b in range(1, B):
                sp.dma_start(x_all[:, b * NT * D:(b + 1) * NT * D].rearrange("p (t d) -> p t d", t=NT),
                             x_in[b].rearrange("(t p) d -> p t d", p=P)).then_inc(s_x, 16)
            sp.wait_ge(s_fill, N_FILLS)
            sp.wait_ge(s_dfill, N_DVE_FILLS)

            def put(b, parts, scratch, names, s, puts, gets, n_get):
                wait_apart(sp, gets, b * (16 * n_get))
                for i, name in enumerate(names):
                    wait_apart(sp, *at(s, name, b, 1))
                    sp.dma_start(scratch[i].rearrange("(c p) t -> p c t", p=P),
                                 parts[i][:, :, :].bitcast(f32)).then_inc(puts, 16)
                wait_apart(sp, puts, b * 32 + 32)

            def get_q(b, par, s, i):
                sp.wait_ge(*at(s, "scores", b, -H))
                for row, hl in enumerate((0, 0, 1)):
                    sp.dma_start(q_stack[par][row * HD:(row + 1) * HD, :, :].bitcast(f32),
                                 scr_q[hl].rearrange("(h d) t -> d h t", d=HD)).then_inc(q_got[i], 16)

            def move_a(b, par):
                put(b, (q_hi, q_lo), scr_q, ("q_hi", "q_lo"), sa, q_put[0], q_got[0], 3)
                get_q(b, par, sa, 0)
                put(b, (k_hi, k_lo), scr_k, ("k_hi", "k_lo"), sa, k_put, k_got, 6)
                for row, hl in enumerate((0, 1, 0)):
                    src = scr_k[hl].rearrange("(h d) t -> d h t", d=HD)
                    rows = ka_stack[par][row * HD:(row + 1) * HD, :, :].bitcast(f32)
                    sp.dma_start(rows[:, :, 0:RB], src[:, :, T - RB:T]).then_inc(k_got, 16)
                    sp.dma_start(rows[:, :, RB:KA_PAD], src[:, :, 0:KA_PAD - RB]).then_inc(k_got, 16)

            run_batches(sp, lambda: move_a(0, 0), lambda b, par, last: None if last else move_a(b + 1, 1 - par))

            def ffn(i):
                s = sf[i]

                def move(b, par):
                    put(b, (q_hi, q_lo), scr_q, ("q_hi", "q_lo"), s, q_put[i + 1], q_got[i + 1], 3)
                    get_q(b, par, s, i + 1)

                def batch(b, par, last):
                    if not last:
                        move(b + 1, 1 - par)
                    if i == 1:
                        sp.wait_ge(*at(s, "x_done", b, 1))
                        sp.dma_start(out[ds(b, 1)].rearrange("o (t p) d -> p (o t) d", p=P),
                                     x_batch(b).rearrange("p (t d) -> p t d", t=NT)).then_inc(s_out, 16)

                run_batches(sp, lambda: move(0, 0), batch)

            ffn(0)
            sp.wait_ge(*at(sf[0], "x_done", B - 1, 1))
            sp.dma_start(st_wqn, b_wqn).then_inc(s_stage, 16)
            sp.dma_start(st_wk, b_wkT).then_inc(s_stage, 16)
            sp.dma_start(st_pe[:, :, 0:W_ABS], b_wkva.rearrange("(c p) n -> p c n", p=P)).then_inc(s_stage, 16)
            sp.dma_start(st_pe[:, :, W_ABS:], b_wqp.rearrange("(c p) n -> p c n", p=P)).then_inc(s_stage, 16)
            sp.dma_start(st_wv, b_wvT).then_inc(s_stage, 16)
            sp.dma_start(st_wo, b_wo.rearrange("(h p) n -> p h n", p=P)).then_inc(s_stage, 16)
            sp.wait_ge(*at(sm, "x_done", B - 1, 1))
            ffn(1)
            sp.wait_ge(s_out, 16 * B)

        @blk.gpsimd
        def _(pool):
            g = nc.gpsimd
            for s in (sa, sf[0], sm):
                for name, n in s["per"].items():
                    if n:
                        pool.sem_inc(s[name], n)
            g.memset(expo[:, :], -0.5).then_inc(s_fill, 1)
            for i in range(2):
                g.memset(q_stack[i][:, :, :].bitcast(f32), 0.0).then_inc(s_fill, 1)
                g.memset(ka_stack[i][:, :, :].bitcast(f32), 0.0).then_inc(s_fill, 1)
                g.memset(kf_stack[i][:, :].bitcast(f32), 0.0).then_inc(s_fill, 1)
            pool.wait_ge(s_fill, N_FILLS)
            pool.wait_ge(s_dfill, N_DVE_FILLS)
            pool.wait_ge(s_const, 48)

            def residual(s, b, src, ready):
                pool.wait_ge(*ready)
                g.tensor_tensor(x_batch(b), x_batch(b), src, ALU.add).then_inc(s["x_done"], 1)

            y_flat = y[:, :, :].rearrange("p t d -> p (t d)")

            def sums_a(b, q):
                r1, r2, f, hi, lo = (rot1, rot2, q_f, q_hi, q_lo) if q else (krot1, krot2, k_f, k_hi, k_lo)
                n = "q" if q else "k"
                pool.wait_ge(*at(sa, n + "_rot1", b, 1))
                pool.wait_ge(*at(sa, n + "_rot2", b, 1))
                pool.wait_ge(*at(sa, n + "_hi", b, 0))
                if q:
                    pool.wait_ge(*at(sa, "q_last", b, 0))
                else:
                    pool.wait_ge(*at(sa, "e_ps", b, 0))
                g.tensor_tensor(f, r1, r2, ALU.add).then_inc(sa["q_f"] if q else sa["k_f"], 1)
                pool.wait_ge(*at(sa, n + "_hi", b, 1))
                pool.wait_ge(q_put[0] if q else k_put, b * 32)
                g.tensor_tensor(lo[:, :, :], f, hi[:, :, :].bitcast(f32), ALU.subtract)\
                    .then_inc(sa["q_lo"] if q else sa["k_lo"], 1)

            def first_a(b):
                pool_rstd(sa, b)
                pool.wait_ge(*at(sa, "x_hi", b, 1))
                g.tensor_tensor(x_lo[:, :, :], hT[:, :, :], x_hi[:, :, :].bitcast(f32), ALU.subtract)\
                    .then_inc(sa["x_lo"], 1)
                sums_a(b, True)
                sums_a(b, False)

            def batch_a(b, par, last):
                if not last:
                    first_a(b + 1)
                residual(sa, b, guard_z, at(sa, "guarded", b, 6))

            run_batches(pool, lambda: first_a(0), batch_a)
            pool.wait_ge(*at(sa, "x_done", B - 1, 1))

            def ffn(s):
                def batch(b, par, last):
                    if not last:
                        pool_rstd(s, b + 1)
                    residual(s, b, y_flat, at(s, "y", b, 3 * H // G))
                run_batches(pool, lambda: pool_rstd(s, 0), batch)

            ffn(sf[0])

            def first_b(b):
                pool_rstd(sm, b)
                wait_apart(pool, *at(sm, "kva", b, 3))
                g.tensor_scalar(rms[:, :], sq_sum[:, :], 1.0 / LORA, EPS_RMS, ALU.mult, ALU.add).then_inc(sm["rms"], 1)
                pool.wait_ge(*at(sm, "rms", b, 1))
                g.tensor_tensor(rms[:, :], rms[:, :], expo[:, :], ALU.pow).then_inc(sm["rms"], 1)
                for i in range(4):
                    t, hh = i // 2, i % 2
                    pool.wait_ge(*at(sm, "qr_dve", b, i + 1))
                    pool.wait_ge(*at(sm, "qT_ps", b, 0))
                    g.tensor_tensor(q_tok[:, t, hh * 8:(hh + 1) * 8, LORA:P],
                                    rope1[:, :, :].rearrange("p c (e d) -> p (c e) d", d=ROPE),
                                    rope2[:, :, :].rearrange("p c (e d) -> p (c e) d", d=ROPE),
                                    ALU.add).then_inc(sm["qr_out"], 1)

            run_batches(pool, lambda: first_b(0), lambda b, par, last: None if last else first_b(b + 1))
            pool.wait_ge(*at(sm, "x_done", B - 1, 1))
            ffn(sf[1])


        @blk.scalar
        def _(act):
            a = nc.scalar
            act.wait_ge(s_w, 64)
            a.activation(a_hi[:, :, :], st_a, ACT.Copy).then_inc(s_split, 1)
            a.activation(f_hi[:, :, :], st_f, ACT.Copy).then_inc(s_split, 1)
            act.wait_ge(s_fill, N_FILLS)
            act.wait_ge(s_dfill, N_DVE_FILLS)
            act.wait_ge(s_arena, N_ARENA)

            def exps(s, b, h):
                act.wait_ge(*at(s, "maxed", b, h + 1))
                if s["kind"] == "a":
                    g, j = h // G, h % G
                    if j == 0:
                        act.wait_ge(*at(s, "small_ps", b, g - 1))
                    for t in range(NT):
                        last = a.activation(pg[:, g % 2, t, j, 0:KA], s_guard[:, h % 2, t, 0:KA], ACT.Exp,
                                            scale=-1.0, bias=neg_max[:, h % 4, t:t + 1])
                else:
                    act.wait_ge(*at(s, "pT_ps", b, h - 3))
                    bank = ps_s[slot_of(h)] if s["kind"] == "f" else ps_s[h % 2]
                    for t, (lo, n) in enumerate(((0, P), (2 * P if s["kind"] == "f" else P, 2 * P))):
                        kw = dict(accum_out=sums[:, h % 4, t:t + 1]) if s["kind"] == "b" else {}
                        last = a.activation(probs[:, h % 4, t * P:t * P + n], bank[:, lo:lo + n], ACT.Exp,
                                            bias=neg_max[:, h % 4, t:t + 1], **kw)
                last.then_inc(s["exp"], 1)

            def heads(s, b, par, last, n, step):
                for h in range(H):
                    if h + 1 < H:
                        exps(s, b, h + 1)
                    elif not last:
                        exps(s, b + 1, 0)
                    if not last:
                        step(b + 1, 1 - par, h)
                    if on_act(s, h):
                        copy_probs(act, s, b, h, n, 2 if s["kind"] == "b" else G)
                    if s["kind"] == "b":
                        if h % 2 == 0 and h > 0:
                            act_ctx(b, h // 2 - 1)
                    elif h % G == 1 and h > G:
                        act_oT(s, b, h // G - 1)
                if s["kind"] != "b":
                    act_oT(s, b, H // G - 1)

            def first_a(b, par, h):
                if h == 2:
                    act.wait_ge(*at(sa, "hT", b, 2))
                    a.activation(x_hi[:, :, :], hT[:, :, :], ACT.Copy).then_inc(sa["x_hi"], 1)
                elif h == 5:
                    act.wait_ge(*at(sa, "v_ps", b, 0))
                    a.activation(rep_hi[:, :, :].rearrange("p c (g k) -> p c g k", g=G),
                                 hT[:, :, 0:VC].unsqueeze(2).to_broadcast([P, NC, G, VC]),
                                 ACT.Copy).then_inc(sa["rep"], 1)
                elif h in (6, 8):
                    n, f, hi, puts = ("q", q_f, q_hi, q_put[0]) if h == 6 else ("k", k_f, k_hi, k_put)
                    act.wait_ge(*at(sa, n + "_f", b, 1))
                    act.wait_ge(*at(sa, n + "_lo", b, 0))
                    act.wait_ge(puts, b * 32)
                    a.activation(hi[:, :, :], f, ACT.Copy).then_inc(sa[n + "_hi"], 1)
                elif h == 9:
                    act.wait_ge(*at(sa, "e_dve", b, 3))
                    for i, (lo, hi) in enumerate(((0, 1), (1, RB), (RB, KA))):
                        a.activation(e_row[0:H, lo:hi], e_row[0:H, lo:hi], ACT.Exp, scale=-1.0,
                                     bias=e_s[0:H, 2:3], accum_out=e_s[0:H, 3 + i:4 + i]).then_inc(sa["e_exp"], 1)
                elif h == 12:
                    act.wait_ge(*at(sa, "v_ps", b, 1))
                    a.activation(v_big[par][:, :, 0:HD], halves(ps_a)[:, 1, :].rearrange("p (h d) -> p h d", h=H),
                                 ACT.Copy).then_inc(sa["v_big"], 1)

            def start(s, step):
                for h in range(H):
                    step(0, 0, h)
                exps(s, 0, 0)

            def batch_a(b, par, last):
                heads(sa, b, par, last, T, first_a)
                act.wait_ge(*at(sa, "yT_ps", b, 1))
                a.activation(yT, halves(ps_t[0]), ACT.Copy).then_inc(sa["yT"], 1)

            run_batches(act, lambda: start(sa, first_a), batch_a)
            act.wait_ge(*at(sa, "x_done", B - 1, 1))

            def ffn(s, i):
                def step(b, par, h):
                    if h == 2:
                        act_x_hi(s, b)
                    elif h == 3:
                        act.wait_ge(*at(s, "q_ps", b, 1))
                        act.wait_ge(q_put[i + 1], b * 32)
                        a.activation(q_hi[:, :, :], halves(ps_b), ACT.Copy).then_inc(s["q_hi"], 1)
                    elif h == 5:
                        act.wait_ge(*at(s, "gate", b, 4))
                        a.activation(g_e, g_d, ACT.Exp).then_inc(s["gate_exp"], 1)
                    elif h == 9:
                        act.wait_ge(*at(s, "kT_ps", b, 1))
                        a.activation(kf_stack[par][0:3 * HD, :], ps_b[0:3 * HD, 0:T], ACT.Copy).then_inc(s["k_stack"], 1)

                run_batches(act, lambda: start(s, step), lambda b, par, last: heads(s, b, par, last, 3 * P, step))
                act.wait_ge(*at(s, "x_done", B - 1, 1))

            ffn(sf[0], 0)

            act.wait_ge(s_stage, 16 * 6)
            a.activation(wb_hi[:, :, 0:W_ABS], st_pe[:, :, 0:W_ABS], ACT.Copy).then_inc(b_hi, 1)
            a.activation(wb_hi[:, :, W_PE:W_COLS], st_pe[:, :, W_ABS:], ACT.Copy).then_inc(b_hi, 1)
            for i in range(4):
                act.wait_ge(b_prep, i + 1)
                a.activation(wb_hi[:, i // 2, W_ABS + (i % 2) * 512:W_ABS + (i % 2 + 1) * 512], ps[i][:, :],
                             ACT.Copy).then_inc(b_hi, 1)

            def act_ctx(b, p):
                act.wait_ge(*at(sm, "o_ps", b, p + 1))
                act.wait_ge(*at(sm, "wo_ps", b, p - 1))
                a.activation(oT[:, p % 2, :], halves(ps_o)[:, p % 2, :], ACT.Copy).then_inc(sm["oT"], 1)

            def step_b(b, par, h):
                if h == 2:
                    act_x_hi(sm, b)
                for i in Q_SLOTS.get(h, ()):
                    if i % 2 == 0:
                        t, hh = i // 4, i // 2 % 2
                        act.wait_ge(*at(sm, "qa_ps", b, i // 2 + 1))
                        act.wait_ge(*at(sm, "qT_ps", b, 0))
                        a.activation(q_tok[:, t, hh * 8:(hh + 1) * 8, 0:LORA],
                                     ps_a[:, :].rearrange("p (h d) -> p h d", h=8), ACT.Copy).then_inc(sm["qa_out"], 1)
                if h == 9:
                    act.wait_ge(*at(sm, "kT_ps", b, 1))
                    a.activation(kbT[par][:, :], ps_a[:, 0:T], ACT.Copy, scale=SCALE_B).then_inc(sm["kT"], 1)
                for i in QT_SLOTS.get(h, ()):
                    if i % 2 == 0:
                        act.wait_ge(*at(sm, "qT_ps", b, i + 1))
                        a.activation(qT[par][:, 2 * i:2 * i + 2, :], halves(ps_b), ACT.Copy).then_inc(sm["qT_act"], 1)

            def batch_b(b, par, last):
                heads(sm, b, par, last, 3 * P, step_b)
                act_ctx(b, H // 2 - 1)

            run_batches(act, lambda: start(sm, step_b), batch_b)
            act.wait_ge(*at(sm, "x_done", B - 1, 1))
            ffn(sf[1], 1)

        @blk.vector
        def _(dve):
            v = nc.vector

            def link(s, name, b, n, ins, fixed=False):
                ins.then_inc(s[name], 1)
                if fixed:
                    wait_apart(dve, *at(s, name, b, n))
                else:
                    dve.wait_ge(*at(s, name, b, n))

            for m in v_sh:
                v.memset(m[:, :, :], 0.0).then_inc(s_dfill, 1)
            v.memset(big_pos[:, :], BIG)
            v.memset(big_neg[:, :], -BIG)
            dve.wait_ge(s_dfill, 2)
            dve.wait_ge(s_const, 48)
            for m in v_sh:
                v.memset(m[:, :, HD:HD + 1], 1.0).then_inc(s_dfill, 1)
            v.tensor_copy(ident_bf[:, :], ident).then_inc(s_dfill, 1)
            v.tensor_copy(mask_bf[:, :], cst[:, C_MASK:C_MASK + P]).then_inc(s_dfill, 1)
            dve.wait_ge(s_split, 2)
            v.tensor_tensor(a_lo[:, :, :], st_a, a_hi[:, :, :].bitcast(f32), ALU.subtract).then_inc(s_split, 1)
            v.tensor_tensor(f_lo[:, :, :], st_f, f_hi[:, :, :].bitcast(f32), ALU.subtract).then_inc(s_split, 1)
            dve.wait_ge(s_split, 4)
            v.memset(psm, 0.0).then_inc(s_arena, 1)
            for i in range(2):
                v.memset(v_big[i], 0.0).then_inc(s_arena, 1)
                v.memset(v_blk[i], 0.0).then_inc(s_arena, 1)
            dve.wait_ge(s_arena, 5)
            for i in range(2):
                v.memset(v_big[i][:, :, HD:HD + 1], 1.0).then_inc(s_arena, 1)
                for j in range(G):
                    v.memset(v_blk[i][j * VC:(j + 1) * VC, :, j, HD:HD + 1], 1.0).then_inc(s_arena, 1)
            dve.wait_ge(s_arena, N_ARENA)
            dve.wait_ge(s_fill, N_FILLS)
            dve.wait_ge(s_dfill, N_DVE_FILLS)

            def maxima(s, b, h):
                dve.wait_ge(*at(s, "scores", b, h + 1))
                for t in range(NT):
                    nm = neg_max[:, h % 4, t:t + 1]
                    if s["kind"] == "a":
                        if t == 0:
                            dve.wait_ge(*at(s, "exp", b, h - 1))
                        last = v.tensor_scalar(s_guard[:, h % 2, t, 0:KA], halves(ps_s[slot_of(h)])[:, t, 0:KA],
                                               FLT_MAX, FLT_MAX, ALU.min, ALU.min, accum_out=nm)
                    else:
                        lo = (0, 2 * P if s["kind"] == "f" else P)[t]
                        bank = ps_s[slot_of(h)] if s["kind"] == "f" else ps_s[h % 2]
                        last = v.tensor_reduce(nm, bank[:, lo:lo + (t + 1) * P], AX.X, ALU.max, negate=True)
                last.then_inc(s["maxed"], 1)

            def normalize_probs(b, h):
                dve.wait_ge(*at(sm, "exp", b, h + 1))
                link(sm, "normed", b, 2 * h + 1, v.reciprocal(inv_sum[:, h % 4, :], sums[:, h % 4, :]))
                for t, (lo, n) in enumerate(((0, P), (P, 2 * P))):
                    p = probs[:, h % 4, lo:lo + n]
                    last = v.tensor_scalar(p, p, inv_sum[:, h % 4, t:t + 1], None, ALU.mult)
                last.then_inc(sm["normed"], 1)

            def heads(s, b, par, last, n, step):
                for h in range(H):
                    if h + 1 < H:
                        maxima(s, b, h + 1)
                    elif not last:
                        maxima(s, b + 1, 0)
                    if s["kind"] == "b":
                        normalize_probs(b, h)
                    if not last:
                        step(b + 1, 1 - par, h)
                    if s["kind"] == "a" and h % G == G - 1:
                        g = h // G
                        dve.wait_ge(*at(s, "exp", b, h + 1))
                        dve.wait_ge(*at(s, "small_ps", b, g - 1))
                        v.tensor_copy(psm[:, g % 2, :, :].rearrange("p t (j k) -> p t j k", j=G)[:, :, :, 0:SB],
                                      pg[:, g % 2, :, :, RB:KA]).then_inc(s["small_in"], 1)
                    if not on_act(s, h):
                        copy_probs(dve, s, b, h, n, G)
                    if s["kind"] == "a" and h % G == G - 1:
                        g = h // G
                        dve.wait_ge(*at(s, "small_ps", b, g + 1))
                        dve.wait_ge(*at(s, "o_ps", b, g - 1))
                        v.tensor_copy(psmT[:, g % 2, :], ps_o[:, T:2 * T]).then_inc(s["small"], 1)
                    if s["kind"] != "b" and h % G == 2 and h > G:
                        divide(s, b, h // G - 1)
                if s["kind"] != "b":
                    divide(s, b, H // G - 1)

            def divide(s, b, g):
                if g == 0:
                    dve.wait_ge(*at(s, "x_done", b, 0))
                dve_divide(s, b, g)

            def start(s, step):
                for h in range(H):
                    step(0, 0, h)
                maxima(s, 0, 0)

            def step_a(b, par, h):
                if h == 0:
                    dve_stats(sa, b)
                elif h == 1:
                    dve_normalize(sa, b)
                elif h == 2:
                    dve.wait_ge(*at(sa, "xT", b, 1))
                    link(sa, "hT", b, 1, v.tensor_scalar(guard_t, ps_a[:, :], 0.0, BIG, ALU.max, ALU.min))
                    v.scalar_tensor_tensor(hT[:, :, :].rearrange("p c t -> p (c t)"), ps_a[:, :], 0.0, guard_t,
                                           op0=ALU.min, op1=ALU.add).then_inc(sa["hT"], 1)
                elif h in (4, 5, 6, 7):
                    n = "q" if h < 6 else "k"
                    r, bank = ((rot1, rot2) if h < 6 else (krot1, krot2))[h % 2], (ps_b, ps_a)[h % 2]
                    table = ((C_COS, C_SIN), (C_COSK, C_SINK))[h >= 6][h % 2]
                    dve.wait_ge(*at(sa, n + ("_ps", "r_ps")[h % 2], b, 1))
                    dve.wait_ge(*at(sa, n + "_f", b, 0))
                    v.tensor_tensor(r, halves(bank), cst[:, table:table + T].unsqueeze(1).to_broadcast([P, NC, T]),
                                    ALU.mult).then_inc(sa[n + ("_rot1", "_rot2")[h % 2]], 1)
                    if h == 7:
                        dve.wait_ge(*at(sa, "q_f", b, 1))
                        for c in range(NC):
                            v.tensor_scalar(q_bd[:, c, :], cst[:, C_HM + c * H:C_HM + (c + 1) * H],
                                            q_f[:, c, T - 1:T], None, ALU.mult).then_inc(sa["q_last"], 1)
                elif h == 8:
                    dve.wait_ge(*at(sa, "v_ps", b, 0))
                    dve.wait_ge(*at(sa, "x_lo", b, 1))
                    v.tensor_copy(rep_lo[:, :, :].rearrange("p c (g k) -> p c g k", g=G),
                                  x_lo[:, :, 0:VC].bitcast(f32).unsqueeze(2).to_broadcast([P, NC, G, VC])
                                  ).then_inc(sa["rep"], 1)
                elif h == 9:
                    dve.wait_ge(*at(sa, "e_ps", b, 1))
                    e = [e_s[0:H, i:i + 1] for i in range(16)]
                    v.tensor_scalar(e_row[0:H, 0:RB], ps_b[0:H, T - RB:T], FLT_MAX, FLT_MAX, ALU.min, ALU.min,
                                    accum_out=e[0]).then_inc(sa["e_dve"], 1)
                    link(sa, "e_dve", b, 2,
                         v.tensor_scalar(e_row[0:H, RB:KA], ps_b[0:H, 0:SB], FLT_MAX, FLT_MAX, ALU.min, ALU.min,
                                         accum_out=e[1]))
                    v.tensor_tensor(e[2], e[0], e[1], ALU.min).then_inc(sa["e_dve"], 1)
                elif h == 10:
                    dve.wait_ge(*at(sa, "e_exp", b, 3))
                    e = [e_s[0:H, i:i + 1] for i in range(16)]
                    step_n = lambda n, ins: link(sa, "e_dve", b, n, ins)
                    step_n(4, v.scalar_tensor_tensor(e[6], e[3], e[4], e[5], op0=ALU.add, op1=ALU.add))
                    step_n(5, v.reciprocal(e[7], e[6]))
                    step_n(6, v.tensor_tensor(e[8], e[3], e[7], ALU.mult))
                    step_n(7, v.tensor_tensor(e[9], e[4], e[7], ALU.mult))
                    step_n(8, v.tensor_scalar(e[10], e[9], 1.0 / (T - E_TOK - 1), 1e-6, ALU.mult, ALU.add))
                    step_n(9, v.reciprocal(e[11], e[10]))
                    step_n(10, v.tensor_tensor(e[12], e[8], e[11], ALU.mult))
                    step_n(11, v.tensor_scalar(e[13], e[12], 0.0, 1.0, ALU.max, ALU.min))
                    step_n(12, v.tensor_tensor(e[14], cst16[:, D + P:D + P + 1], e[13], ALU.is_lt))
                    v.scalar_tensor_tensor(b_row[0:H, :], ps_b[0:H, T:2 * T], e[14], cst16[:, 0:D],
                                           op0=ALU.mult, op1=ALU.mult).then_inc(sa["e_dve"], 1)
                elif h == 12:
                    dve.wait_ge(*at(sa, "v_big", b, 1))
                    for j in range(G):
                        rows = slice(j * VC, (j + 1) * VC)
                        last = v.tensor_copy(v_blk[par][rows, :, j, 0:HD],
                                             ps_a[rows, 0:D].rearrange("p (g j d) -> p g j d", g=G, j=G)[:, :, j, :])
                    last.then_inc(sa["v_small"], 1)

            def batch_a(b, par, last):
                heads(sa, b, par, last, T, step_a)
                dve.wait_ge(*at(sa, "wo_ps", b, 1))
                dve.wait_ge(*at(sa, "x_done", b, 0))
                m = inf_m.bitcast(i32)
                step_n = lambda n, ins, fixed=False: link(sa, "guarded", b, n, ins, fixed)
                step_n(1, v.tensor_scalar(guard_t, ps_t[1][:, :], 0.0, None, ALU.max))
                step_n(2, v.scalar_tensor_tensor(guard_z, ps_t[1][:, :], 0.0, guard_t, op0=ALU.min, op1=ALU.add))
                step_n(3, v.tensor_scalar(m, guard_z, FLT_MAX, None, ALU.is_gt), True)
                step_n(4, v.copy_predicated(guard_z, m, big_pos[:, :].to_broadcast([P, NT * D])))
                step_n(5, v.tensor_scalar(m, guard_z, -FLT_MAX, None, ALU.is_lt), True)
                v.copy_predicated(guard_z, m, big_neg[:, :].to_broadcast([P, NT * D])).then_inc(sa["guarded"], 1)

            dve.wait_ge(s_x, 16 * B)
            run_batches(dve, lambda: start(sa, step_a), batch_a)
            dve.wait_ge(*at(sa, "x_done", B - 1, 1))

            def ffn(s, i):
                def step(b, par, h):
                    if h == 0:
                        dve_stats(s, b)
                    elif h == 1:
                        dve_normalize(s, b)
                    elif h == 2:
                        dve_x_lo(s, b)
                    elif h == 4:
                        dve.wait_ge(*at(s, "q_hi", b, 1))
                        dve.wait_ge(q_put[i + 1], b * 32)
                        v.tensor_tensor(q_lo[:, :, :], halves(ps_b), q_hi[:, :, :].bitcast(f32),
                                        ALU.subtract).then_inc(s["q_lo"], 1)
                    elif h == 5:
                        dve.wait_ge(*at(s, "kg1_ps", b, 1))
                        gate = lambda n, ins: link(s, "gate", b, n, ins)
                        v.tensor_copy(lg[:, 0, :], ps_a[:, D:D + H]).then_inc(s["gate"], 1)
                        gate(2, v.tensor_copy(lg[:, 1, :], ps_b[:, D:D + H]))
                        gate(3, v.tensor_reduce(g_s[:, :, 0], lg, AX.X, ALU.max))
                        top = g_s[:, :, 0:1].to_broadcast([P, NT, H])
                        v.tensor_tensor(g_d, lg, top, ALU.subtract).then_inc(s["gate"], 1)
                        gate(5, v.tensor_tensor(g_eq, lg, top, ALU.is_equal))
                        gate(6, v.tensor_tensor(g_eq, g_eq, cst[:, C_DESC:C_DESC + H].unsqueeze(1)
                                                .to_broadcast([P, NT, H]), ALU.mult))
                        gate(7, v.tensor_reduce(g_s[:, :, 1], g_eq, AX.X, ALU.max))
                        gate(8, v.tensor_tensor(g_hot, g_eq, g_s[:, :, 1:2].to_broadcast([P, NT, H]), ALU.is_equal))
                    elif h == 6:
                        for t, bank in enumerate((ps_a, ps_b)):
                            v.tensor_tensor(g_pick[:, t, :].rearrange("p (h d) -> p h d", h=H),
                                            bank[:, 0:D].rearrange("p (h d) -> p h d", h=H),
                                            g_hot[:, t, :].unsqueeze(2).to_broadcast([P, H, HD]),
                                            ALU.mult).then_inc(s["k_sel"], 1)
                        dve.wait_ge(*at(s, "k_sel", b, 2))
                        link(s, "k_sel", b, 3,
                             v.tensor_reduce(kv_sh, g_pick.rearrange("p t (h d) -> p t d h", h=H), AX.X, ALU.add))
                        scale = HD ** -0.5
                        dve.wait_ge(*at(s, "kT_ps", b, 0))
                        link(s, "k48", b, 1, v.tensor_scalar(k48[:, :, 0:HD], kv_sh, scale, None, ALU.mult))
                        v.scalar_tensor_tensor(k48[:, :, HD:2 * HD], kv_sh, scale, k48[:, :, 0:HD].bitcast(f32),
                                               op0=ALU.mult, op1=ALU.subtract).then_inc(s["k48"], 1)
                        v.tensor_copy(k48[:, :, 2 * HD:3 * HD], k48[:, :, 0:HD].bitcast(f32)).then_inc(s["k48"], 1)
                        dve.wait_ge(*at(s, "gate_exp", b, 1))
                        gate = lambda n, ins: link(s, "gate", b, n, ins)
                        gate(9, v.tensor_reduce(g_s[:, :, 2], g_e, AX.X, ALU.add))
                        gate(10, v.reciprocal(g_s[:, :, 3], g_s[:, :, 2]))
                        gate(11, v.tensor_tensor(g_hotv, g_hot, g_s[:, :, 3:4].to_broadcast([P, NT, H]), ALU.mult))
                    elif h == 8:
                        dve.wait_ge(*at(s, "v_ps", b, 1))
                        link(s, "v_sel", b, 1,
                             v.tensor_tensor(g_pick.rearrange("p t (h d) -> p t h d", h=H),
                                             halves(ps_a).rearrange("p t (h d) -> p t h d", h=H),
                                             g_hotv.unsqueeze(3).to_broadcast([P, NT, H, HD]), ALU.mult))
                        v.tensor_reduce(v_sh[par][:, :, 0:HD], g_pick.rearrange("p t (h d) -> p t d h", h=H), AX.X,
                                        ALU.add).then_inc(s["v_sel"], 1)

                run_batches(dve, lambda: start(s, step), lambda b, par, last: heads(s, b, par, last, 3 * P, step))
                dve.wait_ge(*at(s, "x_done", B - 1, 1))

            ffn(sf[0], 0)

            dve.wait_ge(s_stage, 16 * 6)
            dve.wait_ge(b_hi, 2)
            v.tensor_tensor(wb_lo[:, :, 0:W_ABS], st_pe[:, :, 0:W_ABS], wb_hi[:, :, 0:W_ABS].bitcast(f32),
                            ALU.subtract).then_inc(b_lo, 1)
            v.tensor_tensor(wb_lo[:, :, W_PE:W_COLS], st_pe[:, :, W_ABS:], wb_hi[:, :, W_PE:W_COLS].bitcast(f32),
                            ALU.subtract).then_inc(b_lo, 1)
            for i in range(4):
                dve.wait_ge(b_hi, i + 3)
                part = slice(W_ABS + (i % 2) * 512, W_ABS + (i % 2 + 1) * 512)
                v.tensor_tensor(wb_lo[:, i // 2, part], ps[i][:, :], wb_hi[:, i // 2, part].bitcast(f32),
                                ALU.subtract).then_inc(b_lo, 1)
            for i in range(4):
                dve.wait_ge(b_prep, i + 5)
                v.tensor_copy(m_vo[:, 2 * i:2 * i + 2, :], halves(ps[4 + i])).then_inc(b_mvo, 1)

            def rotary(dst, src, cos, sin, heads_dim):
                hr = ROPE // 2
                shape = [P, heads_dim, ROPE]
                tab = lambda c: c if c.shape[1] == heads_dim and len(c.shape) == 3 else \
                    c.unsqueeze(1).to_broadcast(shape)
                cos, sin = tab(cos), tab(sin)
                v.tensor_tensor(dst[0], src, cos, ALU.mult)
                v.tensor_tensor(dst[1][:, :, 0:hr], src[:, :, hr:ROPE], sin[:, :, 0:hr], ALU.mult)
                return v.tensor_tensor(dst[1][:, :, hr:ROPE], src[:, :, 0:hr], sin[:, :, hr:ROPE], ALU.mult)

            cosb = cst[:, C_COSB:C_COSB + NT * ROPE].rearrange("p (t d) -> p t d", t=NT)
            sinb = cst[:, C_SINB:C_SINB + NT * ROPE].rearrange("p (t d) -> p t d", t=NT)

            def step_b(b, par, h):
                if h == 0:
                    dve_stats(sm, b)
                elif h == 1:
                    dve_normalize(sm, b)
                elif h == 2:
                    dve_x_lo(sm, b)
                elif h == 3:
                    dve.wait_ge(*at(sm, "kva_ps", b, 1))
                    link(sm, "kva", b, 1, v.tensor_copy(kva_tok[:, :, :], halves(ps_b)[:, :, 0:W_ABS]))
                    for t in range(NT):
                        lat = kva_tok[:, t, 0:LORA]
                        v.tensor_tensor_reduce(out=k_rot[:, 0, t, :], in0=lat, in1=lat, scale=1.0, scalar=0.0,
                                               op0=ALU.mult, op1=ALU.add,
                                               accum_out=sq_sum[:, t:t + 1]).then_inc(sm["kva"], 1)
                elif h == 5:
                    dve.wait_ge(*at(sm, "kva", b, 3))
                    link(sm, "k_tok", b, 1, rotary((k_rot[:, 0], k_rot[:, 1]), kva_tok[:, :, LORA:W_ABS],
                                                   cosb, sinb, NT))
                    v.tensor_tensor(kv_tok[par][:, :, LORA:W_ABS], k_rot[:, 0], k_rot[:, 1], ALU.add)
                    dve.wait_ge(*at(sm, "rms", b, 2))
                    for t in range(NT):
                        last = v.scalar_tensor_tensor(kv_tok[par][:, t, 0:LORA], kva_tok[:, t, 0:LORA],
                                                      rms[:, t:t + 1], norm_bc[:, :], op0=ALU.mult, op1=ALU.mult)
                    last.then_inc(sm["k_tok"], 1)
                for i in Q_SLOTS.get(h, ()):
                    if i % 2 == 1:
                        dve.wait_ge(*at(sm, "qr_ps", b, i // 2 + 1))
                        dve.wait_ge(*at(sm, "qr_out", b, i // 2))
                        rotary([r[:, :, :].rearrange("p c (e d) -> p (c e) d", d=ROPE) for r in (rope1, rope2)],
                               ps_b[:, :].rearrange("p (h d) -> p h d", h=8), cosb[:, i // 4, :], sinb[:, i // 4, :],
                               8).then_inc(sm["qr_dve"], 1)
                for i in QT_SLOTS.get(h, ()):
                    if i % 2 == 1:
                        dve.wait_ge(*at(sm, "qT_ps", b, i + 1))
                        v.tensor_copy(qT[par][:, 2 * i:2 * i + 2, :], halves(ps_a)).then_inc(sm["qT_dve"], 1)

            def batch_b(b, par, last):
                heads(sm, b, par, last, 3 * P, step_b)
                dve.wait_ge(*at(sm, "wo_ps", b, H // 2))
                v.tensor_tensor(x_batch(b), ps_s[2][:, :], x_batch(b), ALU.add).then_inc(sm["x_done"], 1)

            run_batches(dve, lambda: start(sm, step_b), batch_b)
            dve.wait_ge(*at(sm, "x_done", B - 1, 1))
            ffn(sf[1], 1)

        @blk.tensor
        def _(pe):
            mm, transpose = nc.tensor.matmul, nc.tensor.transpose
            pe.wait_ge(s_split, 4)
            pe.wait_ge(s_fill, N_FILLS)
            pe.wait_ge(s_dfill, N_DVE_FILLS)
            pe.wait_ge(s_arena, N_ARENA)
            pe.wait_ge(s_w, 64)

            def mask(out_ap, stop=True):
                return mm(out_ap, ident_bf[:, :], mask_bf[:, :], start=False, stop=True, skip_group_check=True)

            def scores(s, b, par, h, i=0):
                if s["kind"] == "a":
                    if h == 0:
                        pe.wait_ge(q_got[0], b * 48 + 48)
                        pe.wait_ge(k_got, b * 96 + 96)
                    pe.wait_ge(*at(s, "maxed", b, before(h)))
                    for t in range(NT):
                        last = mm(halves(ps_s[slot_of(h)])[:, t, 0:KA_PAD], q_stack[par][:, h, t * P:(t + 1) * P],
                                  ka_stack[par][:, h, :], start=True, stop=True)
                elif s["kind"] == "f":
                    if h == 0:
                        pe.wait_ge(q_got[i + 1], b * 48 + 48)
                        pe.wait_ge(*at(s, "k_stack", b, 1))
                    pe.wait_ge(*at(s, "exp", b, before(h)))
                    for t in range(NT):
                        o = halves(ps_s[slot_of(h)])[:, t, :]
                        mm(o, q_stack[par][:, h, t * P:(t + 1) * P], kf_stack[par][:, :], start=True, stop=True)
                        last = mask(o[:, t * P:(t + 1) * P])
                else:
                    if h == 0:
                        pe.wait_ge(*at(s, "kT", b, 1))
                    if h % 2 == 0:
                        pe.wait_ge(*at(s, "qT_dve" if h // 2 % 2 else "qT_act", b, h // 4 + 1))
                    pe.wait_ge(*at(s, "exp", b, h - 1))
                    for t in range(NT):
                        o = ps_s[h % 2][:, t * P:t * P + (t + 1) * P]
                        mm(o, qT[par][:, h, t * P:(t + 1) * P], kbT[par][:, 0:(t + 1) * P], start=True, stop=True)
                        last = mask(o[:, t * P:(t + 1) * P])
                last.then_inc(s["scores"], 1)

            def heads(s, b, par, last, step, i=0):
                for h in range(H):
                    if h + 2 < H:
                        scores(s, b, par, h + 2, i)
                    elif not last:
                        scores(s, b + 1, 1 - par, h + 2 - H, i)
                    if not last:
                        step(b + 1, 1 - par, h)
                    if s["kind"] == "a":
                        pe.wait_ge(*at(s, "exp", b, h + 1))
                        if h == 1:
                            pe.wait_ge(*at(s, "guarded", b, -4))
                        pe_transpose_probs(s, b, h, [pg[:, h // G % 2, t, h % G, 0:P] for t in range(NT)])
                        if h % G == G - 1:
                            g = h // G
                            pe.wait_ge(*at(s, "y", b, 3 * g))
                            pe.wait_ge(*at(s, "small_in", b, g + 1))
                            for t in range(NT):
                                tr = transpose(ps_o[:, T + t * P:T + (t + 1) * P],
                                               psm[:, g % 2, t, :], ident)
                            tr.then_inc(s["small_ps"], 1)
                        if h % G == 0 and h:
                            outputs_a(b, par, h // G - 1)
                    elif s["kind"] == "f":
                        pe.wait_ge(*at(s, "exp", b, h + 1))
                        pe_transpose_probs(s, b, h, [probs[:, h % 4, k * P:(k + 1) * P] for k in range(3)])
                        if h % G == 0 and h:
                            outputs_f(s, b, par, h // G - 1)
                    else:
                        pe.wait_ge(*at(s, "normed", b, 2 * h + 2))
                        pe_transpose_probs(s, b, h, [probs[:, h % 4, k * P:(k + 1) * P] for k in range(3)])
                        if h % 2 == 0 and h:
                            attend_b(b, par, h // 2 - 1)
                        if h % 2 == 1 and h > 2:
                            project_b(b, (h - 3) // 2)
                    if s["kind"] != "b" and h % G == 2 and h > G:
                        pe_untranspose(s, b, h // G - 1)

            def outputs_a(b, par, g):
                pe_wait_copies(sa, b, g * G, G)
                pe.wait_ge(*at(sa, "small", b, g + 1))
                pe.wait_ge(*at(sa, "y", b, 3 * g))
                if g == 0:
                    pe.wait_ge(*at(sa, "v_big", b, 1))
                    pe.wait_ge(*at(sa, "v_small", b, 1))
                mm(ps_o[:, 0:T], v_blk[par][:, g, :, :].rearrange("p j c -> p (j c)"), psmT[:, g % 2, :], start=True, stop=False,
                   skip_group_check=True)
                for j in range(G):
                    h = g * G + j
                    last = mm(ps_o[j * VC:(j + 1) * VC, 0:T], v_big[par][:, h, :], probsT[:, h % 8, 0:T],
                              start=False, stop=True, skip_group_check=True)
                last.then_inc(sa["o_ps"], 1)

            def outputs_f(s, b, par, g):
                pe_wait_copies(s, b, g * G, G)
                pe.wait_ge(*at(s, "y", b, 3 * g))
                if g == 0:
                    pe.wait_ge(*at(s, "v_sel", b, 2))
                for k, (lo, n) in enumerate(((0, T), (T, P))):
                    for j in range(G):
                        last = mm(ps_o[j * VC:(j + 1) * VC, T - n:T], v_sh[par][:, k, :],
                                  probsT[:, (g * G + j) % 8, lo:lo + n], start=k == 0, stop=k == 1,
                                  skip_group_check=True)
                last.then_inc(s["o_ps"], 1)

            def start(s, step, i=0):
                for h in range(H):
                    step(0, 0, h)
                scores(s, 0, 0, 0, i)
                scores(s, 0, 0, 1, i)

            def step_a(b, par, h):
                if h == 1:
                    pe.wait_ge(*at(sa, "v_big", b, 0))
                    pe.wait_ge(*at(sa, "v_small", b, 0))
                    pe_transpose_x(sa, b)
                elif h in (3, 4, 5, 6):
                    n = ("q_ps", "qr_ps", "k_ps", "kr_ps")[h - 3]
                    if h == 3:
                        pe.wait_ge(*at(sa, "x_lo", b, 1))
                        pe.wait_ge(*at(sa, "e_dve", b, 0))
                    elif h > 4:
                        pe.wait_ge(*at(sa, ("q_rot1", "q_rot2")[h - 5], b, 1))
                    bank = (ps_a, ps_b)[h % 2]
                    for c in range(NC):
                        last = mm3(halves(bank)[:, c, :], cols(AW, (h - 3) * D + c * P, P), cols(X, 0, T))
                    last.then_inc(sa[n], 1)
                elif h == 8:
                    pe.wait_ge(*at(sa, "k_f", b, 1))
                    pe.wait_ge(*at(sa, "q_last", b, 2))
                    for c in range(NC):
                        mm(ps_b[0:H, 0:T], q_bd[:, c, :], k_f[:, c, :], start=c == 0, stop=c == NC - 1)
                    tok = tuple((lambda c, w=w: w[:, c, E_TOK:E_TOK + 1].to_broadcast([P, P])) for w in X)
                    mm3(ps_b[:, T:2 * T], tok, cols(AW, 4 * D, D)).then_inc(sa["e_ps"], 1)
                elif h == 11:
                    pe.wait_ge(*at(sa, "k_rot2", b, 1))
                    pe.wait_ge(*at(sa, "e_dve", b, 13))
                    pe.wait_ge(*at(sa, "rep", b, 2))
                    mm3(ps_a[:, 0:D], cols((rep_hi, rep_lo), 0, P), cols(AW, 4 * D, D))
                    mm3(ps_a[:, D:2 * D], cols(X, P, P), cols(AW, 4 * D, D), stop=False)
                    mm(ps_a[:, D:2 * D], cst16[:, D:D + P], b_row[0:H, :], start=False, stop=True)\
                        .then_inc(sa["v_ps"], 1)

            def batch_a(b, par, last):
                heads(sa, b, par, last, step_a)
                outputs_a(b, par, H // G - 1)
                pe_untranspose(sa, b, H // G - 1)
                pe.wait_ge(*at(sa, "y", b, 3 * H // G))
                pe.wait_ge(*copied(sa, b, H - 2, False))
                for c in range(NC):
                    for t in range(NT):
                        last_t = transpose(halves(ps_t[0])[:, c, t * P:(t + 1) * P], y[:, t, c * P:(c + 1) * P], ident)
                last_t.then_inc(sa["yT_ps"], 1)
                pe.wait_ge(*at(sa, "yT", b, 1))
                for t in range(NT):
                    for c in range(NC):
                        last_t = mm(halves(ps_t[1])[:, t, :], yT[:, c, t * P:(t + 1) * P], wo_a[:, c, :],
                                    start=c == 0, stop=c == NC - 1)
                last_t.then_inc(sa["wo_ps"], 1)

            run_batches(pe, lambda: start(sa, step_a), batch_a)
            pe.wait_ge(*at(sa, "x_done", B - 1, 1))

            def ffn(s, i):
                def step(b, par, h):
                    if h == 1:
                        pe.wait_ge(*at(s, "v_sel", b, 0))
                        pe_transpose_x(s, b)
                    elif h == 3:
                        pe.wait_ge(*at(s, "x_lo", b, 1))
                        pe.wait_ge(*at(s, "k_stack", b, 0))
                        for c in range(NC):
                            last = mm3(halves(ps_b)[:, c, :], cols(FW, c * P, P), cols(X, 0, T))
                        last.then_inc(s["q_ps"], 1)
                        mm3(ps_a[:, 0:D + H], cols(X, 0, P), cols(FW, F_KG, D + H)).then_inc(s["kg0_ps"], 1)
                    elif h == 5:
                        pe.wait_ge(*at(s, "q_lo", b, 1))
                        mm3(ps_b[:, 0:D + H], cols(X, P, P), cols(FW, F_KG, D + H)).then_inc(s["kg1_ps"], 1)
                    elif h == 7:
                        pe.wait_ge(*at(s, "k_sel", b, 2))
                        for t in range(NT):
                            last = mm3(halves(ps_a)[:, t, :], cols(X, t * P, P), cols(FW, F_V, D))
                        last.then_inc(s["v_ps"], 1)
                        wait_apart(pe, *at(s, "k48", b, 3))
                        for t in range(NT):
                            last = transpose(ps_b[0:3 * HD, t * P:(t + 1) * P], k48[:, t, :].bitcast(f32), ident)
                        last.then_inc(s["kT_ps"], 1)

                def batch(b, par, last):
                    heads(s, b, par, last, step, i)
                    outputs_f(s, b, par, H // G - 1)
                    pe_untranspose(s, b, H // G - 1)

                run_batches(pe, lambda: start(s, step, i), batch)
                pe.wait_ge(*at(s, "x_done", B - 1, 1))

            ffn(sf[0], 0)

            pe.wait_ge(s_stage, 16 * 6)
            for i in range(4):
                for k in range(8):
                    h = (i % 2) * 8 + k
                    last = mm(ps[i][:, k * LORA:(k + 1) * LORA], st_wqn[:, h, (i // 2) * P:(i // 2 + 1) * P],
                              st_wk[:, h, :], start=True, stop=True)
                last.then_inc(b_prep, 1)
            for i in range(4):
                for r in range(2):
                    for j in range(2):
                        h = (2 * i + r) * 2 + j
                        last = mm(ps[4 + i][j * LORA:(j + 1) * LORA, r * D:(r + 1) * D], st_wv[:, h, :],
                                  st_wo[:, h, :], start=True, stop=True)
                last.then_inc(b_prep, 1)
            pe.wait_ge(b_lo, 6)
            pe.wait_ge(b_mvo, 4)

            def attend_b(b, par, p):
                pe_wait_copies(sm, b, 2 * p, 2)
                pe.wait_ge(*at(sm, "oT", b, p))
                for k, (lo, n) in enumerate(((0, T), (T, P))):
                    for j in range(2):
                        last = mm(halves(ps_o)[j * LORA:(j + 1) * LORA, p % 2, T - n:T], kv_tok[par][:, k, 0:LORA],
                                  probsT[:, (2 * p + j) % 8, lo:lo + n], start=k == 0, stop=k == 1,
                                  skip_group_check=True)
                last.then_inc(sm["o_ps"], 1)

            def project_b(b, p):
                pe.wait_ge(*at(sm, "oT", b, p + 1))
                if p == 0:
                    pe.wait_ge(*at(sm, "x_done", b, 0))
                for t in range(NT):
                    last = mm(halves(ps_s[2])[:, t, :], oT[:, p % 2, t * P:(t + 1) * P], m_vo[:, p, :],
                              start=p == 0 and t == 0, stop=p == H // 2 - 1, skip_group_check=True)
                last.then_inc(sm["wo_ps"], 1)

            def step_b(b, par, h):
                if h == 1:
                    pe.wait_ge(*at(sm, "qT_dve", b, 0))
                    pe_transpose_x(sm, b)
                elif h == 3:
                    pe.wait_ge(*at(sm, "x_lo", b, 1))
                    pe.wait_ge(*at(sm, "qT_act", b, 0))
                    for t in range(NT):
                        last = mm3(halves(ps_b)[:, t, 0:192], cols(X, t * P, P), cols(WB, 0, 192))
                    last.then_inc(sm["kva_ps"], 1)
                for i in Q_SLOTS.get(h, ()):
                    t, hh, rot = i // 4, i // 2 % 2, i % 2
                    if rot:
                        pe.wait_ge(*at(sm, "kva", b, 1))
                        pe.wait_ge(*at(sm, "qr_dve", b, i // 2))
                    else:
                        pe.wait_ge(*at(sm, "qa_out", b, i // 2))
                    mm3((ps_a, ps_b)[rot][:, :], cols(X, t * P, P), cols(WB, (W_ABS, W_PE)[rot] + hh * 512, 512))\
                        .then_inc((sm["qa_ps"], sm["qr_ps"])[rot], 1)
                if h == 9:
                    pe.wait_ge(*at(sm, "qa_out", b, 4))
                    pe.wait_ge(*at(sm, "k_tok", b, 2))
                    for t in range(NT):
                        last = transpose(ps_a[:, t * P:(t + 1) * P], kv_tok[par][:, t, :], ident)
                    last.then_inc(sm["kT_ps"], 1)
                for i in QT_SLOTS.get(h, ()):
                    pe.wait_ge(*at(sm, "qr_out", b, 4))
                    if i % 2:
                        pe.wait_ge(*at(sm, "kT", b, 1))
                        pe.wait_ge(*at(sm, "qT_dve", b, i // 2))
                    else:
                        pe.wait_ge(*at(sm, "qr_dve", b, 4))
                        pe.wait_ge(*at(sm, "qT_act", b, i // 2))
                    for j in range(2):
                        for t in range(NT):
                            last = transpose(halves((ps_b, ps_a)[i % 2])[:, j, t * P:(t + 1) * P],
                                             q_tok[:, t, 2 * i + j, :], ident)
                    last.then_inc(sm["qT_ps"], 1)

            def batch_b(b, par, last):
                heads(sm, b, par, last, step_b)
                attend_b(b, par, H // 2 - 1)
                project_b(b, H // 2 - 1)

            run_batches(pe, lambda: start(sm, step_b), batch_b)
            pe.wait_ge(*at(sm, "x_done", B - 1, 1))
            ffn(sf[1], 1)


def constants():
    import numpy as np

    f = np.float32
    c = np.zeros((P, C_END), f)
    c[:, C_ID:C_ID + P] = np.eye(P, dtype=f)
    c[:, C_MASK:C_MASK + P] = np.where(np.arange(P)[None, :] > np.arange(P)[:, None], f(-1e30), f(0))
    pos = np.arange(T, dtype=f)
    inv = (f(1.0) / f(10000.0) ** (np.arange(0, HD, 2, dtype=f) / f(HD))).astype(f)
    ang = pos[None, :] * inv[:, None]
    ang = np.tile(np.concatenate([ang, ang]), (P // HD, 1)).astype(f)
    sign = np.tile(np.repeat(np.array([-1, 1], f), HD // 2), P // HD)[:, None]
    k_scale = f(-(HD ** -0.5))
    for lo, table in ((C_COS, np.cos(ang)), (C_SIN, np.sin(ang) * sign), (C_COSK, np.cos(ang) * k_scale),
                      (C_SINK, np.sin(ang) * sign * k_scale)):
        c[:, lo:lo + T] = table
    for t in range(NC):
        for p in range(P):
            c[p, C_HM + t * H + (t * P + p) // HD] = 1
    c[:, C_DESC:C_DESC + H] = H - np.arange(H, dtype=f)
    inv = (f(1.0) / f(10000.0) ** (np.arange(0, ROPE, 2, dtype=f) / f(ROPE))).astype(f)
    ang = (pos[:, None] * inv[None, :]).astype(f).reshape(NT, P, ROPE // 2).transpose(1, 0, 2)
    cos, sin = np.cos(ang), np.sin(ang)
    c[:, C_COSB:C_COSB + NT * ROPE] = np.concatenate([cos, cos], 2).reshape(P, -1)
    c[:, C_SINB:C_SINB + NT * ROPE] = np.concatenate([-sin, sin], 2).reshape(P, -1)
    c16 = np.zeros((H, D + P), f)
    for h in range(H):
        c16[h, h * HD:(h + 1) * HD] = 1
    c16[:, D + 1:] = f(1.0 / RB)
    return c, c16


def kernel(**inputs):
    import numpy as np
    import concourse.bacc as bacc
    from concourse import mybir
    from concourse.bass_utils import run_bass_kernel_spmd

    w = {k: np.asarray(v) for k, v in inputs.items()}
    turned = (np.arange(D) // HD) * HD + (np.arange(D) % HD + HD // 2) % HD
    wq, wk, wv = (w[f"L0_attn_a_w{n}"] for n in "qkv")
    qkv, gate = w["L0_ffn_W_qkv"], w["L0_ffn_W_gate"]
    bq = w["L0_attn_b_wq"].reshape(D, H, QH)
    bkv = w["L0_attn_b_wkv_b"].reshape(LORA, H, NOPE + VD)
    consts, consts16 = constants()
    arrays = {
        "x": w["L0_attn_a_hidden_states"],
        "a_wT": np.concatenate([wq, wq[turned], wk, wk[turned], wv]).T,
        "a_woT": w["L0_attn_a_wo"].T,
        "a_u": w["L0_attn_a_bern_u"].T,
        "f_wT": np.concatenate([qkv[0:D], qkv[2 * D:], qkv[D:2 * D], gate]).T,
        "b_wqn": bq[:, :, 0:NOPE].transpose(2, 1, 0),
        "b_wqp": bq[:, :, NOPE:].reshape(D, H * ROPE),
        "b_wkT": bkv[:, :, 0:NOPE].transpose(2, 1, 0),
        "b_wvT": bkv[:, :, NOPE:].transpose(2, 1, 0),
        "b_wo": w["L0_attn_b_wo"],
        "b_wkva": w["L0_attn_b_wkv_a"],
        "b_norm": w["L0_attn_b_kv_norm_scale"],
        "consts": consts,
        "consts16": consts16,
    }
    arrays = {k: np.ascontiguousarray(v) for k, v in arrays.items()}
    nc = bacc.Bacc("TRN2", target_bir_lowering=False, num_devices=1)
    args = [nc.dram_tensor(k, v.shape, mybir.dt.from_np(v.dtype), kind="ExternalInput").ap()
            for k, v in arrays.items()]
    out = nc.dram_tensor("out", (B, T, D), mybir.dt.float32, kind="ExternalOutput").ap()
    hybrid_layers_kernel(nc, *args, out)
    r = run_bass_kernel_spmd(nc, [arrays], core_ids=[0])
    return r.results[0]["out"]
```

```python
from contextlib import ExitStack

import concourse.bass as bass
from concourse import mybir

B, T, D, H = 8, 256, 256, 16
P = 128
NT = T // P
NC = D // P
HD = D // H
NOPE, ROPE, VD, LORA = 128, 64, 128, 64
QH = NOPE + ROPE
SB, RB = T // 10, T // 2
E_TOK = T - RB
KA = SB + RB
KA_PAD = RB + 64
G = 4
VC = 32
STK = 96
ARENA = 12544
N_FILLS, N_DVE_FILLS = 7, 6
N_ARENA = 15
FLT_MAX = 3.4028234663852886e38
BIG = 1.0e4
EPS_LN, EPS_RMS = 1e-5, 1e-6
SCALE_B = QH ** -0.5
C_ID, C_MASK = 0, P
C_COS, C_SIN, C_COSK, C_SINK = 2 * P, 2 * P + T, 2 * P + 2 * T, 2 * P + 2 * T + KA_PAD
C_HM = C_SINK + KA_PAD
C_DESC = C_HM + NC * H
C_COSB = C_DESC + H
C_SINB = C_COSB + NT * ROPE
C_END = C_SINB + NT * ROPE
F_V, F_K, F_G = D, 2 * D, 3 * D
F_COLS = 3 * D + H
TX = T + KA_PAD - RB
A_COLS = 5 * D
W_KVA = NOPE
W_ABS = LORA + ROPE
W_PE = W_ABS + H * LORA
W_COLS = W_PE + H * ROPE


PV_SLOT, BACK_SLOT, DIVIDE_SLOT = 5, 6, 7
YT_SLOTS, WO_SLOTS, GUARD_SLOTS = (4, 5), (6, 8), (9, 10, 11, 12)
Q_SLOTS = {4: (0, 1), 5: (2,), 6: (3, 4), 7: (5,), 8: (6, 7)}
QT_SLOTS = {10: (0, 1), 11: (2,), 12: (3, 4), 13: (5,), 14: (6,), 15: (7,)}


def lead(kind):
    return 1 if kind == "b" else 2


def slot_of(h):
    return 1 if h == H - 1 else h % 3


def before(h):
    for back in range(h - 1, h - H - 1, -1):
        if slot_of(back % H) == slot_of(h):
            return back + 1


def hybrid_layers_kernel(nc, x_in, a_wT, a_woT, a_u, f_wT, b_wqn, b_wqp, b_wkT, b_wvT, b_wo, b_wkva,
                         b_norm, consts, consts16, out):
    f32, f32r, bf16, i32 = mybir.dt.float32, mybir.dt.float32r, mybir.dt.bfloat16, mybir.dt.int32
    ALU = mybir.AluOpType
    ACT = mybir.ActivationFunctionType
    AX = mybir.AxisListType
    ds = bass.ds

    ctx = ExitStack()
    with ctx:
        def sb(name, shape, dt=f32, stack=ctx):
            return stack.enter_context(nc.sbuf_tensor(name, shape, dt))

        def sem(name):
            return ctx.enter_context(nc.semaphore(name))

        x_all = sb("x_all", [P, B * NT * D])
        cst = sb("cst", [P, C_END])
        cst16 = sb("cst16", [H, D + P + 1])
        ident_bf = sb("ident_bf", [P, P], bf16)
        mask_bf = sb("mask_bf", [P, P], bf16)
        big_pos = sb("big_pos", [P, 1])
        big_neg = sb("big_neg", [P, 1])
        expo = sb("expo", [P, NT])
        stats = sb("stats", [P, NT, 6])
        mv = sb("mv", [P, NT, 2])
        var_eps = sb("var_eps", [P, NT])
        rstd = sb("rstd", [P, NT])
        xn = sb("xn", [P, NT, D])
        rope1 = sb("rope1", [P, NC, T])
        x_hi = sb("x_hi", [P, NC, TX], f32r)
        x_lo = sb("x_lo", [P, NC, TX], f32r)
        f_hi = sb("f_hi", [P, NC, F_COLS], f32r)
        f_lo = sb("f_lo", [P, NC, F_COLS], f32r)
        q_hi = sb("q_hi", [P, NC, T], f32r)
        q_lo = sb("q_lo", [P, NC, T], f32r)
        q_stack = [sb(f"q_stack{i}", [STK, H, T], f32r) for i in range(2)]
        kf_stack = [sb(f"kf_stack{i}", [STK, T], f32r) for i in range(2)]
        v_sh = [sb(f"v_sh{i}", [P, NT, VC]) for i in range(2)]
        neg_max = sb("neg_max", [P, 4, NT])
        sums = sb("sums", [P, 4, NT])
        inv_sum = sb("inv_sum", [P, 4, NT])
        probs = sb("probs", [P, 4, 3 * P])
        probsT = sb("probsT", [P, 8, 3 * P])
        oT = sb("oT", [P, 2, T])
        recip = sb("recip", [P, 2, NT, G])
        y = sb("y", [P, NT, D])
        k48 = sb("k48", [P, NT, 3 * HD], f32r)
        norm_bc = sb("norm_bc", [P, LORA])
        sq_sum = sb("sq_sum", [P, NT])
        rms = sb("rms", [P, NT])
        arena = sb("arena", [P, ARENA])

        ident = cst[:, C_ID:C_ID + P]
        ps = [ctx.enter_context(nc.psum_tensor(f"bank{i}", [P, 512], f32)) for i in range(8)]
        ps_s, ps_t, ps_o, ps_a, ps_b = ps[0:3], ps[3:5], ps[5], ps[6], ps[7]

        scr_q = [nc.dram_tensor(f"scr_q{i}", [D, T], f32, kind="Internal").ap() for i in range(2)]
        scr_k = [nc.dram_tensor(f"scr_k{i}", [D, KA_PAD], f32, kind="Internal").ap() for i in range(2)]


        s_const = sem("constants_loaded")
        s_x = sem("x_loaded")
        s_w = sem("small_weights_loaded")
        s_fill = sem("pool_fills_done")
        s_dfill = sem("dve_fills_done")
        s_arena = sem("arena_initialised")
        s_split = sem("small_weights_split")
        s_stage = sem("attn_b_weights_staged")
        s_out = sem("out_stored")
        q_put = [sem(f"q_put{i}") for i in range(3)]
        q_got = [sem(f"q_got{i}") for i in range(3)]
        k_put, k_got = sem("k_put"), sem("k_got")
        b_prep, b_hi, b_lo, b_mvo = sem("b_prep"), sem("b_hi"), sem("b_lo"), sem("b_mvo")

        ON_ACT = {"a": (1, 4, 5, 9, 10, 13, 14), "f": (1, 2, 4, 5, 7, 8, 10, 11, 13, 14), "b": tuple(range(H))}

        def signals(layer, kind, **own):
            n_act = len(ON_ACT[kind])
            per = dict(stats=4, rstd=2, xn=1, xT=1, x_hi=1, x_lo=1, scores=H, maxed=H, exp=H, pT_ps=H,
                       copy_dve=H - n_act, copy_act=n_act, oT=2 * H // G if kind == "b" else H // G,
                       o_ps=2 * H // G if kind == "b" else H // G, x_done=1, **own)
            return dict(kind=kind, per=per, past=0, **{n: sem(f"{layer}_{n}") for n in per})

        HEADS16 = dict(r_ps=H // G, y=3 * H // G, q_hi=1, q_lo=1)
        sa = signals("attn_a", "a", **HEADS16, hT=3, q_ps=1, qr_ps=1, q_rot1=1, q_rot2=1, q_f=1, k_ps=1, kr_ps=1,
                     k_rot1=1, k_rot2=1, k_f=1, k_hi=1, k_lo=1, q_last=2, e_ps=1, e_dve=11, e_exp=3, v_ps=1,
                     v_big=1, v_small=1, small_in=H // G, rep=2, yT_ps=NC, yT=NC, wo_ps=NT, guarded=8)
        sf = [signals("ffn", "f", **HEADS16, q_ps=1, gate_ps=1, k_ps=1, v_ps=1, gate=10, gate_exp=1, k_sel=2,
                      k48=3, kT_ps=1, k_stack=1, v_sel=2)]
        sf.append({**sf[0], "past": B})
        sm = signals("attn_b", "b", kva_ps=1, kva=3, rms=2, k_tok=2, kT_ps=1, kT=1, qa_ps=4, qa_out=4, qr_ps=4,
                     qr_dve=4, qr_out=4, qT_ps=8, qT_act=4, qT_dve=4, normed=2 * H, wo_ps=H // 2)

        def at(s, name, b, n):
            per = s["per"][name]
            return s[name], b * per + ((s["past"] + 1) * per + n)

        def wait_apart(eng, signal, value):
            value = value if isinstance(value, int) else eng.to_reg(value)
            eng.wait_ge(s_const, 48)
            eng.wait_ge(signal, value)

        def late_group(b, h, slot, first, work):
            g, rest = divmod(h - slot, G)
            if rest == 0:
                if g >= 0:
                    work(b, g)
                elif not first:
                    work(b - 1, g + H // G)

        def copied(s, b, h, act):
            if h < 0:
                b, h = b - 1, h + H
            return at(s, "copy_act" if act else "copy_dve", b,
                      sum((k in ON_ACT[s["kind"]]) == act for k in range(h + 1)))

        def on_act(s, h):
            return h % H in ON_ACT[s["kind"]]

        def x_tile(b, t):
            return x_all[:, ds(b * (NT * D) + t * D, D)]

        def x_batch(b):
            return x_all[:, ds(b * (NT * D), NT * D)]

        def halves(p):
            return p[:, :].rearrange("p (t d) -> p t d", t=2)

        scope_a, scope_b = ExitStack(), ExitStack()
        a_hi = sb("a_hi", [P, NC, A_COLS], f32r, scope_a)
        a_lo = sb("a_lo", [P, NC, A_COLS], f32r, scope_a)
        wo_a = sb("wo_a", [P, NC, D], f32, scope_a)
        ka_stack = [sb(f"ka_stack{i}", [STK, H, KA_PAD], f32r, scope_a) for i in range(2)]
        k_hi = sb("k_hi", [P, NC, KA_PAD], f32r, scope_a)
        k_lo = sb("k_lo", [P, NC, KA_PAD], f32r, scope_a)
        rep_hi = sb("rep_hi", [P, NC, P], f32r, scope_a)
        rep_lo = sb("rep_lo", [P, NC, P], f32r, scope_a)
        scope_a.close()
        wb_hi = sb("wb_hi", [P, NC, W_COLS], f32r, scope_b)
        wb_lo = sb("wb_lo", [P, NC, W_COLS], f32r, scope_b)
        m_vo = sb("m_vo", [P, H // 2, D], f32, scope_b)
        kva_tok = sb("kva_tok", [P, NT, W_ABS], f32, scope_b)
        kv_tok = [sb(f"kv_tok{i}", [P, NT, W_ABS], f32, scope_b) for i in range(2)]
        kbT = [sb(f"kbT{i}", [P, T], f32, scope_b) for i in range(2)]
        k_rot = sb("k_rot", [P, 2, NT, ROPE], f32, scope_b)
        scope_b.close()

        def cut(*shapes):
            lo, views = 0, []
            for shape in shapes:
                n = 1
                for k in shape:
                    n *= k
                v, names = arena[:, lo:lo + n], "abcd"[:len(shape)]
                if len(shape) > 1:
                    v = v.rearrange(f"p ({' '.join(names)}) -> p {' '.join(names)}",
                                    **{k: m for k, m in zip(names[1:], shape[1:])})
                views.append(v)
                lo += n
            assert lo <= ARENA
            return views

        st_a, st_f = cut((NC, A_COLS), (NC, F_COLS))
        (pg, s_guard, rot1, rot2, krot1, krot2, q_f, k_f, v_big0, v_big1, v_blk0, v_blk1, psmT, e_row, e_s, q_bd,
         b_row, yT, guard_t, guard_z, inf_m, psm, hT) = cut(
            (2, NT, G, 160), (2, NT, 160), (NC, T), (NC, T), (NC, KA_PAD), (NC, KA_PAD), (NC, T), (NC, KA_PAD),
            (H, VC), (H, VC), (G, G, VC), (G, G, VC), (2, T), (KA,), (16,), (NC, H), (D,), (NC, T), (NT * D,),
            (NT * D,), (NT * D,), (2, NT, P), (NC, TX))
        v_big, v_blk = [v_big0, v_big1], [v_blk0, v_blk1]
        lg, g_s, g_d, g_e, g_eq, g_hot, g_hotv, g_pick, kv_sh = cut(
            (NT, H), (NT, 4), (NT, H), (NT, H), (NT, H), (NT, H), (NT, H), (NT, D), (NT, HD))
        st_wqn, st_wo, st_wk, st_wv, st_pe = cut((H, D), (H, D), (H, LORA), (H, LORA), (NC, W_ABS + H * ROPE))
        qT0, qT1, q_tok = cut((H, T), (H, T), (NT, H, P))
        qT = [qT0, qT1]
        rope2 = y

        X, AW, FW, WB = (x_hi, x_lo), (a_hi, a_lo), (f_hi, f_lo), (wb_hi, wb_lo)

        def cols(pair, lo, n):
            return tuple((lambda c, w=w: w[:, c, lo:lo + n]) for w in pair)

        def mm3(out_ap, lhs, rhs, stop=True):
            (lh, ll), (rh, rl) = lhs, rhs
            steps = [(l, r, c) for c in range(NC) for l, r in ((lh, rh), (lh, rl), (ll, rh))]
            for i, (l, r, c) in enumerate(steps):
                last = nc.tensor.matmul(out_ap, l(c), r(c), start=i == 0, stop=stop and i == len(steps) - 1)
            return last

        def run_batches(eng, first, body):
            first()
            body(0, 0, True, False)
            with eng.Fori(0, B // 2 - 1) as pair:
                b = pair * 2 + 1
                body(b, 1, False, False)
                body(b + 1, 0, False, False)
            body(B - 1, 1, False, True)

        def dve_stats(s, b):
            v = nc.vector
            for t in range(NT):
                v.bn_stats(stats[:, t, :], x_tile(b, t)).then_inc(s["stats"], 1)
            wait_apart(v, *at(s, "stats", b, 2))
            for t in range(NT):
                v.bn_aggr(mv[:, t, :], stats[:, t, :]).then_inc(s["stats"], 1)

        def pool_rstd(s, b):
            g = nc.gpsimd
            wait_apart(g, *at(s, "stats", b, 4))
            g.tensor_scalar(var_eps[:, :], mv[:, :, 1], EPS_LN, None, ALU.add).then_inc(s["rstd"], 1)
            g.wait_ge(*at(s, "rstd", b, 1))
            g.tensor_tensor(rstd[:, :], var_eps[:, :], expo[:, :], ALU.pow).then_inc(s["rstd"], 1)

        def dve_normalize(s, b):
            v = nc.vector
            v.wait_ge(*at(s, "rstd", b, 2))
            v.wait_ge(*at(s, "xT", b, 0))
            for t in range(NT):
                last = v.tensor_scalar(xn[:, t, :], x_tile(b, t), mv[:, t, 0:1], rstd[:, t:t + 1],
                                       ALU.subtract, ALU.mult)
            last.then_inc(s["xn"], 1)

        def pe_transpose_x(s, b):
            nc.tensor.wait_ge(*at(s, "xn", b, 1))
            for c in range(NC):
                for t in range(NT):
                    last = nc.tensor.transpose(halves(ps_a)[:, c, t * P:(t + 1) * P], xn[:, t, c * P:(c + 1) * P],
                                               ident)
            last.then_inc(s["xT"], 1)

        def act_x_hi(s, b):
            nc.scalar.wait_ge(*at(s, "xT", b, 1))
            nc.scalar.activation(x_hi[:, :, 0:T], halves(ps_a), ACT.Copy).then_inc(s["x_hi"], 1)

        def dve_x_lo(s, b):
            nc.vector.wait_ge(*at(s, "x_hi", b, 1))
            nc.vector.tensor_tensor(x_lo[:, :, 0:T], halves(ps_a), x_hi[:, :, 0:T].bitcast(f32),
                                    ALU.subtract).then_inc(s["x_lo"], 1)

        def pe_transpose_probs(s, b, h, blocks, more=None):
            pe = nc.tensor
            pe.wait_ge(*copied(s, b, h - 2, on_act(s, h - 2)))
            if more:
                more(ps_t[h % 2][:, T:2 * T])
            for i, block in enumerate(blocks):
                last = pe.transpose(ps_t[h % 2][:, i * P:(i + 1) * P], block, ident)
            last.then_inc(s["pT_ps"], 1)

        def copy_probs(eng, s, b, h, n, group, more=None):
            act = on_act(s, h)
            eng.wait_ge(*at(s, "pT_ps", b, h + 1))
            if more:
                more(ps_t[h % 2][:, T:2 * T])
            eng.wait_ge(*at(s, "o_ps", b, h // group + 1 - 8 // group))
            if act:
                nc.scalar.activation(probsT[:, h % 8, 0:n], ps_t[h % 2][:, 0:n], ACT.Copy).then_inc(s["copy_act"], 1)
            else:
                nc.vector.tensor_copy(probsT[:, h % 8, 0:n], ps_t[h % 2][:, 0:n]).then_inc(s["copy_dve"], 1)

        def pe_wait_copies(s, b, h0, n):
            for act in (True, False):
                mine = [h for h in range(h0, h0 + n) if on_act(s, h) == act]
                if mine:
                    nc.tensor.wait_ge(*copied(s, b, mine[-1], act))

        def pe_untranspose(s, b, g):
            pe = nc.tensor
            pe.wait_ge(*at(s, "oT", b, g + 1))
            pe.wait_ge(*at(s, "y", b, 3 * g))
            for t in range(NT):
                last = pe.transpose(ps_o[:, T + t * P:T + (t + 1) * P], oT[:, g % 2, t * P:(t + 1) * P], ident)
            last.then_inc(s["r_ps"], 1)

        def act_oT(s, b, g):
            act = nc.scalar
            act.wait_ge(*at(s, "o_ps", b, g + 1))
            act.wait_ge(*at(s, "r_ps", b, g - 1))
            act.activation(oT[:, g % 2, :], ps_o[:, 0:T], ACT.Copy).then_inc(s["oT"], 1)

        def dve_divide(s, b, g):
            v = nc.vector
            v.wait_ge(*at(s, "r_ps", b, g + 1))
            r = ps_o[:, T:2 * T].rearrange("p (t g c) -> p t g c", t=NT, g=G)
            v.reciprocal(recip[:, g % 2], r[:, :, :, HD]).then_inc(s["y"], 1)
            v.wait_ge(*at(s, "y", b, 3 * g + 1))
            yv = y[:, :, g * G * HD:(g + 1) * G * HD].rearrange("p t (g d) -> p t g d", g=G)
            for t in range(NT):
                v.tensor_tensor(yv[:, t], r[:, t, :, 0:HD],
                                recip[:, g % 2, t, :].unsqueeze(2).to_broadcast([P, G, HD]),
                                ALU.mult).then_inc(s["y"], 1)

        blk = ctx.enter_context(nc.Block())

        @blk.sync
        def _(sp):
            sp.dma_start(x_all[:, 0:NT * D].rearrange("p (t d) -> p t d", t=NT),
                         x_in[0].rearrange("(t p) d -> p t d", p=P)).then_inc(s_x, 16)
            sp.dma_start(cst[:, :], consts).then_inc(s_const, 16)
            sp.dma_start(cst16[:, 0:D + P], consts16).then_inc(s_const, 16)
            sp.dma_start(cst16[:, D + P:D + P + 1], a_u).then_inc(s_const, 16)
            sp.dma_start(st_a, a_wT.rearrange("(c p) n -> p c n", p=P)).then_inc(s_w, 16)
            sp.dma_start(st_f, f_wT.rearrange("(c p) n -> p c n", p=P)).then_inc(s_w, 16)
            sp.dma_start(wo_a[:, :, :], a_woT.rearrange("(c p) n -> p c n", p=P)).then_inc(s_w, 16)
            sp.dma_start(norm_bc[:, :], b_norm.partition_broadcast(P)).then_inc(s_w, 16)
            for b in range(1, B):
                sp.dma_start(x_all[:, b * NT * D:(b + 1) * NT * D].rearrange("p (t d) -> p t d", t=NT),
                             x_in[b].rearrange("(t p) d -> p t d", p=P)).then_inc(s_x, 16)
            sp.wait_ge(s_fill, N_FILLS)
            sp.wait_ge(s_dfill, N_DVE_FILLS)

            def put(b, parts, scratch, names, s, puts, gets, n_get):
                wait_apart(sp, gets, b * (16 * n_get))
                for i, name in enumerate(names):
                    wait_apart(sp, *at(s, name, b, 1))
                    sp.dma_start(scratch[i].rearrange("(c p) t -> p c t", p=P),
                                 parts[i][:, :, :].bitcast(f32)).then_inc(puts, 16)
                wait_apart(sp, puts, b * 32 + 32)

            def get_q(b, par, s, i):
                sp.wait_ge(*at(s, "scores", b, -H))
                for row, hl in enumerate((0, 0, 1)):
                    sp.dma_start(q_stack[par][row * HD:(row + 1) * HD, :, :].bitcast(f32),
                                 scr_q[hl].rearrange("(h d) t -> d h t", d=HD)).then_inc(q_got[i], 16)

            def move_a(b, par):
                put(b, (k_hi, k_lo), scr_k, ("k_hi", "k_lo"), sa, k_put, k_got, 3)
                sp.wait_ge(*at(sa, "scores", b, -H))
                for row, hl in enumerate((0, 1, 0)):
                    sp.dma_start(ka_stack[par][row * HD:(row + 1) * HD, :, :].bitcast(f32),
                                 scr_k[hl].rearrange("(h d) t -> d h t", d=HD)).then_inc(k_got, 16)
                put(b, (q_hi, q_lo), scr_q, ("q_hi", "q_lo"), sa, q_put[0], q_got[0], 3)
                get_q(b, par, sa, 0)

            run_batches(sp, lambda: move_a(0, 0),
                        lambda b, par, first, last: None if last else move_a(b + 1, 1 - par))

            def ffn(i):
                s = sf[i]

                def move(b, par):
                    put(b, (q_hi, q_lo), scr_q, ("q_hi", "q_lo"), s, q_put[i + 1], q_got[i + 1], 3)
                    get_q(b, par, s, i + 1)

                def store(b):
                    sp.wait_ge(*at(s, "x_done", b, 1))
                    sp.dma_start(out[ds(b, 1)].rearrange("o (t p) d -> p (o t) d", p=P),
                                 x_batch(b).rearrange("p (t d) -> p t d", t=NT)).then_inc(s_out, 16)

                def batch(b, par, first, last):
                    if not last:
                        move(b + 1, 1 - par)
                    if i == 1 and not first:
                        store(b - 1)

                run_batches(sp, lambda: move(0, 0), batch)
                if i == 1:
                    store(B - 1)

            ffn(0)
            sp.wait_ge(*at(sf[0], "x_done", B - 1, 1))
            sp.dma_start(st_wqn, b_wqn).then_inc(s_stage, 16)
            sp.dma_start(st_wk, b_wkT).then_inc(s_stage, 16)
            sp.dma_start(st_pe[:, :, 0:W_ABS], b_wkva.rearrange("(c p) n -> p c n", p=P)).then_inc(s_stage, 16)
            sp.dma_start(st_pe[:, :, W_ABS:], b_wqp.rearrange("(c p) n -> p c n", p=P)).then_inc(s_stage, 16)
            sp.dma_start(st_wv, b_wvT).then_inc(s_stage, 16)
            sp.dma_start(st_wo, b_wo.rearrange("(h p) n -> p h n", p=P)).then_inc(s_stage, 16)
            sp.wait_ge(*at(sm, "x_done", B - 1, 1))
            ffn(1)
            sp.wait_ge(s_out, 16 * B)

        @blk.gpsimd
        def _(pool):
            g = nc.gpsimd
            for s in (sa, sf[0], sm):
                for name, n in s["per"].items():
                    if n:
                        pool.sem_inc(s[name], n)
            g.memset(expo[:, :], -0.5).then_inc(s_fill, 1)
            for i in range(2):
                g.memset(q_stack[i][:, :, :].bitcast(f32), 0.0).then_inc(s_fill, 1)
                g.memset(ka_stack[i][:, :, :].bitcast(f32), 0.0).then_inc(s_fill, 1)
                g.memset(kf_stack[i][:, :].bitcast(f32), 0.0).then_inc(s_fill, 1)
            pool.wait_ge(s_fill, N_FILLS)
            pool.wait_ge(s_dfill, N_DVE_FILLS)
            pool.wait_ge(s_const, 48)

            def residual(s, b, src, ready):
                pool.wait_ge(*ready)
                g.tensor_tensor(x_batch(b), x_batch(b), src, ALU.add).then_inc(s["x_done"], 1)

            y_flat = y[:, :, :].rearrange("p t d -> p (t d)")

            def sums_a(b, q):
                r1, r2, f, hi, lo = (rot1, rot2, q_f, q_hi, q_lo) if q else (krot1, krot2, k_f, k_hi, k_lo)
                n = "q" if q else "k"
                pool.wait_ge(*at(sa, n + "_rot1", b, 1))
                pool.wait_ge(*at(sa, n + "_rot2", b, 1))
                pool.wait_ge(*at(sa, n + "_hi", b, 0))
                if q:
                    pool.wait_ge(*at(sa, "q_last", b, 0))
                else:
                    pool.wait_ge(*at(sa, "e_ps", b, 0))
                g.tensor_tensor(f, r1, r2, ALU.add).then_inc(sa["q_f"] if q else sa["k_f"], 1)
                pool.wait_ge(*at(sa, n + "_hi", b, 1))
                pool.wait_ge(q_put[0] if q else k_put, b * 32)
                g.tensor_tensor(lo[:, :, :], f, hi[:, :, :].bitcast(f32), ALU.subtract)\
                    .then_inc(sa["q_lo"] if q else sa["k_lo"], 1)

            def first_a(b):
                pool_rstd(sa, b)
                pool.wait_ge(*at(sa, "x_hi", b, 1))
                g.tensor_tensor(x_lo[:, :, :], hT[:, :, :], x_hi[:, :, :].bitcast(f32), ALU.subtract)\
                    .then_inc(sa["x_lo"], 1)
                sums_a(b, False)
                sums_a(b, True)

            def residual_a(b):
                residual(sa, b, guard_z, at(sa, "guarded", b, 8))

            def batch_a(b, par, first, last):
                if not last:
                    first_a(b + 1)
                if not first:
                    residual_a(b - 1)

            run_batches(pool, lambda: first_a(0), batch_a)
            residual_a(B - 1)
            pool.wait_ge(*at(sa, "x_done", B - 1, 1))

            def ffn(s):
                def residual_f(b):
                    residual(s, b, y_flat, at(s, "y", b, 3 * H // G))

                def batch(b, par, first, last):
                    if not last:
                        pool_rstd(s, b + 1)
                    if not first:
                        residual_f(b - 1)

                run_batches(pool, lambda: pool_rstd(s, 0), batch)
                residual_f(B - 1)

            ffn(sf[0])

            def first_b(b):
                pool_rstd(sm, b)
                wait_apart(pool, *at(sm, "kva", b, 3))
                g.tensor_scalar(rms[:, :], sq_sum[:, :], 1.0 / LORA, EPS_RMS, ALU.mult, ALU.add).then_inc(sm["rms"], 1)
                pool.wait_ge(*at(sm, "rms", b, 1))
                g.tensor_tensor(rms[:, :], rms[:, :], expo[:, :], ALU.pow).then_inc(sm["rms"], 1)
                for i in range(4):
                    t, hh = i // 2, i % 2
                    pool.wait_ge(*at(sm, "qr_dve", b, i + 1))
                    pool.wait_ge(*at(sm, "qT_ps", b, 0))
                    g.tensor_tensor(q_tok[:, t, hh * 8:(hh + 1) * 8, LORA:P],
                                    rope1[:, :, :].rearrange("p c (e d) -> p (c e) d", d=ROPE),
                                    rope2[:, :, :].rearrange("p c (e d) -> p (c e) d", d=ROPE),
                                    ALU.add).then_inc(sm["qr_out"], 1)

            run_batches(pool, lambda: first_b(0),
                        lambda b, par, first, last: None if last else first_b(b + 1))
            pool.wait_ge(*at(sm, "x_done", B - 1, 1))
            ffn(sf[1])


        @blk.scalar
        def _(act):
            a = nc.scalar
            act.wait_ge(s_w, 64)
            a.activation(a_hi[:, :, :], st_a, ACT.Copy).then_inc(s_split, 1)
            a.activation(f_hi[:, :, :], st_f, ACT.Copy).then_inc(s_split, 1)
            act.wait_ge(s_fill, N_FILLS)
            act.wait_ge(s_dfill, N_DVE_FILLS)
            act.wait_ge(s_arena, N_ARENA)

            def exps(s, b, h):
                act.wait_ge(*at(s, "maxed", b, h + 1))
                if s["kind"] == "a":
                    g, j = h // G, h % G
                    if j == 0:
                        act.wait_ge(*at(s, "pT_ps", b, (g - 1) * G))
                    for t in range(NT):
                        last = a.activation(pg[:, g % 2, t, j, 0:KA], s_guard[:, h % 2, t, 0:KA], ACT.Exp,
                                            scale=-1.0, bias=neg_max[:, h % 4, t:t + 1])
                else:
                    act.wait_ge(*at(s, "pT_ps", b, h - 3))
                    bank = ps_s[slot_of(h)] if s["kind"] == "f" else ps_s[h % 2]
                    for t, (lo, n) in enumerate(((0, P), (2 * P if s["kind"] == "f" else P, 2 * P))):
                        kw = dict(accum_out=sums[:, h % 4, t:t + 1]) if s["kind"] == "b" else {}
                        last = a.activation(probs[:, h % 4, t * P:t * P + n], bank[:, lo:lo + n], ACT.Exp,
                                            bias=neg_max[:, h % 4, t:t + 1], **kw)
                last.then_inc(s["exp"], 1)

            def heads(s, b, par, first, last, n, step):
                for h in range(H):
                    ahead = h + lead(s["kind"])
                    if ahead < H:
                        exps(s, b, ahead)
                    elif not last:
                        exps(s, b + 1, ahead - H)
                    if not last:
                        step(b + 1, 1 - par, h)
                    if on_act(s, h):
                        late = s["kind"] == "a" and h in YT_SLOTS and not first
                        copy_probs(act, s, b, h, n, 2 if s["kind"] == "b" else G,
                                   (lambda half: act_yT(b - 1, YT_SLOTS.index(h), half)) if late else None)
                    if s["kind"] == "b":
                        if h % 2 == 0 and h > 0:
                            act_ctx(b, h // 2 - 1)
                    else:
                        late_group(b, h, PV_SLOT, first, lambda bb, g: act_oT(s, bb, g))

            def act_yT(b, c, half):
                act.wait_ge(*at(sa, "yT_ps", b, c + 1))
                act.wait_ge(*at(sa, "wo_ps", b, 0))
                a.activation(yT[:, c, :], half, ACT.Copy).then_inc(sa["yT"], 1)

            def first_a(b, par, h):
                if h == 2:
                    act.wait_ge(*at(sa, "hT", b, 3))
                    act.wait_ge(*at(sa, "x_lo", b, 0))
                    a.activation(x_hi[:, :, :], hT, ACT.Copy).then_inc(sa["x_hi"], 1)
                elif h == 6:
                    act.wait_ge(*at(sa, "v_ps", b, 0))
                    a.activation(rep_hi[:, :, :].rearrange("p c (g k) -> p c g k", g=G),
                                 hT[:, :, 0:VC].unsqueeze(2).to_broadcast([P, NC, G, VC]),
                                 ACT.Copy).then_inc(sa["rep"], 1)
                elif h in (7, 9):
                    n, f, hi, puts = ("k", k_f, k_hi, k_put) if h == 7 else ("q", q_f, q_hi, q_put[0])
                    act.wait_ge(*at(sa, n + "_f", b, 1))
                    act.wait_ge(*at(sa, n + "_lo", b, 0))
                    act.wait_ge(puts, b * 32)
                    a.activation(hi[:, :, :], f, ACT.Copy).then_inc(sa[n + "_hi"], 1)
                elif h == 11:
                    act.wait_ge(*at(sa, "e_dve", b, 1))
                    for i, (lo, hi) in enumerate(((0, 1), (1, RB), (RB, KA))):
                        a.activation(e_row[0:H, lo:hi], e_row[0:H, lo:hi], ACT.Exp, scale=-1.0,
                                     bias=e_s[0:H, 2:3], accum_out=e_s[0:H, 3 + i:4 + i]).then_inc(sa["e_exp"], 1)
                elif h == 15:
                    act.wait_ge(*at(sa, "v_ps", b, 1))
                    a.activation(v_big[par][:, :, 0:HD], halves(ps_a)[:, 1, :].rearrange("p (h d) -> p h d", h=H),
                                 ACT.Copy).then_inc(sa["v_big"], 1)

            def start(s, step):
                for h in range(H):
                    step(0, 0, h)
                for h in range(lead(s["kind"])):
                    exps(s, 0, h)

            def batch_a(b, par, first, last):
                heads(sa, b, par, first, last, T, first_a)

            run_batches(act, lambda: start(sa, first_a), batch_a)
            act_oT(sa, B - 1, H // G - 1)
            for c in range(NC):
                act_yT(B - 1, c, ps_t[c][:, T:2 * T])
            act.wait_ge(*at(sa, "x_done", B - 1, 1))

            def ffn(s, i):
                def step(b, par, h):
                    if h == 3:
                        act_x_hi(s, b)
                    elif h == 6:
                        act.wait_ge(*at(s, "q_ps", b, 1))
                        act.wait_ge(q_put[i + 1], b * 32)
                        a.activation(q_hi[:, :, :], halves(ps_b), ACT.Copy).then_inc(s["q_hi"], 1)
                    elif h == 7:
                        act.wait_ge(*at(s, "gate", b, 3))
                        a.activation(g_e, g_d, ACT.Exp).then_inc(s["gate_exp"], 1)
                    elif h == 11:
                        act.wait_ge(*at(s, "kT_ps", b, 1))
                        a.activation(kf_stack[par][0:3 * HD, :], ps_b[0:3 * HD, 0:T], ACT.Copy).then_inc(s["k_stack"], 1)

                run_batches(act, lambda: start(s, step),
                            lambda b, par, first, last: heads(s, b, par, first, last, 3 * P, step))
                act_oT(s, B - 1, H // G - 1)
                act.wait_ge(*at(s, "x_done", B - 1, 1))

            ffn(sf[0], 0)

            act.wait_ge(s_stage, 16 * 6)
            a.activation(wb_hi[:, :, 0:W_ABS], st_pe[:, :, 0:W_ABS], ACT.Copy).then_inc(b_hi, 1)
            a.activation(wb_hi[:, :, W_PE:W_COLS], st_pe[:, :, W_ABS:], ACT.Copy).then_inc(b_hi, 1)
            for i in range(4):
                act.wait_ge(b_prep, i + 1)
                a.activation(wb_hi[:, i // 2, W_ABS + (i % 2) * 512:W_ABS + (i % 2 + 1) * 512], ps[i][:, :],
                             ACT.Copy).then_inc(b_hi, 1)

            def act_ctx(b, p):
                act.wait_ge(*at(sm, "o_ps", b, p + 1))
                act.wait_ge(*at(sm, "wo_ps", b, p - 1))
                a.activation(oT[:, p % 2, :], halves(ps_o)[:, p % 2, :], ACT.Copy).then_inc(sm["oT"], 1)

            def step_b(b, par, h):
                if h == 2:
                    act_x_hi(sm, b)
                for i in Q_SLOTS.get(h, ()):
                    if i % 2 == 0:
                        t, hh = i // 4, i // 2 % 2
                        act.wait_ge(*at(sm, "qa_ps", b, i // 2 + 1))
                        act.wait_ge(*at(sm, "qT_ps", b, 0))
                        a.activation(q_tok[:, t, hh * 8:(hh + 1) * 8, 0:LORA],
                                     ps_a[:, :].rearrange("p (h d) -> p h d", h=8), ACT.Copy).then_inc(sm["qa_out"], 1)
                if h == 9:
                    act.wait_ge(*at(sm, "kT_ps", b, 1))
                    a.activation(kbT[par][:, :], ps_a[:, 0:T], ACT.Copy, scale=SCALE_B).then_inc(sm["kT"], 1)
                for i in QT_SLOTS.get(h, ()):
                    if i % 2 == 0:
                        act.wait_ge(*at(sm, "qT_ps", b, i + 1))
                        a.activation(qT[par][:, 2 * i:2 * i + 2, :], halves(ps_b), ACT.Copy).then_inc(sm["qT_act"], 1)

            def batch_b(b, par, first, last):
                heads(sm, b, par, first, last, 3 * P, step_b)
                act_ctx(b, H // 2 - 1)

            run_batches(act, lambda: start(sm, step_b), batch_b)
            act.wait_ge(*at(sm, "x_done", B - 1, 1))
            ffn(sf[1], 1)

        @blk.vector
        def _(dve):
            v = nc.vector

            def link(s, name, b, n, ins, fixed=False):
                ins.then_inc(s[name], 1)
                if fixed:
                    wait_apart(dve, *at(s, name, b, n))
                else:
                    dve.wait_ge(*at(s, name, b, n))

            for m in v_sh:
                v.memset(m[:, :, :], 0.0).then_inc(s_dfill, 1)
            v.memset(big_pos[:, :], BIG)
            v.memset(big_neg[:, :], -BIG)
            dve.wait_ge(s_dfill, 2)
            dve.wait_ge(s_const, 48)
            for m in v_sh:
                v.memset(m[:, :, HD:HD + 1], 1.0).then_inc(s_dfill, 1)
            v.tensor_copy(ident_bf[:, :], ident).then_inc(s_dfill, 1)
            v.tensor_copy(mask_bf[:, :], cst[:, C_MASK:C_MASK + P]).then_inc(s_dfill, 1)
            dve.wait_ge(s_split, 2)
            v.tensor_tensor(a_lo[:, :, :], st_a, a_hi[:, :, :].bitcast(f32), ALU.subtract).then_inc(s_split, 1)
            v.tensor_tensor(f_lo[:, :, :], st_f, f_hi[:, :, :].bitcast(f32), ALU.subtract).then_inc(s_split, 1)
            dve.wait_ge(s_split, 4)
            v.memset(psm, 0.0).then_inc(s_arena, 1)
            for i in range(2):
                v.memset(v_big[i], 0.0).then_inc(s_arena, 1)
                v.memset(v_blk[i], 0.0).then_inc(s_arena, 1)
            dve.wait_ge(s_arena, 5)
            for i in range(2):
                v.memset(v_big[i][:, :, HD:HD + 1], 1.0).then_inc(s_arena, 1)
                for j in range(G):
                    v.memset(v_blk[i][j * VC:(j + 1) * VC, :, j, HD:HD + 1], 1.0).then_inc(s_arena, 1)
            dve.wait_ge(s_arena, N_ARENA)
            dve.wait_ge(s_fill, N_FILLS)
            dve.wait_ge(s_dfill, N_DVE_FILLS)

            def maxima(s, b, h):
                dve.wait_ge(*at(s, "scores", b, h + 1))
                for t in range(NT):
                    nm = neg_max[:, h % 4, t:t + 1]
                    if s["kind"] == "a":
                        if t == 0:
                            dve.wait_ge(*at(s, "exp", b, h - 1))
                        last = v.tensor_scalar(s_guard[:, h % 2, t, 0:KA], halves(ps_s[slot_of(h)])[:, t, 0:KA],
                                               FLT_MAX, FLT_MAX, ALU.min, ALU.min, accum_out=nm)
                    else:
                        lo = (0, 2 * P if s["kind"] == "f" else P)[t]
                        bank = ps_s[slot_of(h)] if s["kind"] == "f" else ps_s[h % 2]
                        last = v.tensor_reduce(nm, bank[:, lo:lo + (t + 1) * P], AX.X, ALU.max, negate=True)
                last.then_inc(s["maxed"], 1)

            def normalize_probs(b, h):
                dve.wait_ge(*at(sm, "exp", b, h + 1))
                link(sm, "normed", b, 2 * h + 1, v.reciprocal(inv_sum[:, h % 4, :], sums[:, h % 4, :]))
                for t, (lo, n) in enumerate(((0, P), (P, 2 * P))):
                    p = probs[:, h % 4, lo:lo + n]
                    last = v.tensor_scalar(p, p, inv_sum[:, h % 4, t:t + 1], None, ALU.mult)
                last.then_inc(sm["normed"], 1)

            def heads(s, b, par, first, last, n, step):
                for h in range(H):
                    ahead = h + lead(s["kind"])
                    if ahead < H:
                        maxima(s, b, ahead)
                    elif not last:
                        maxima(s, b + 1, ahead - H)
                    if s["kind"] == "b":
                        normalize_probs(b, h)
                    if not last:
                        step(b + 1, 1 - par, h)
                    if s["kind"] == "a" and h % G == G - 2:
                        g = h // G
                        dve.wait_ge(*at(s, "exp", b, h + 2))
                        dve.wait_ge(*at(s, "pT_ps", b, (g - 1) * G))
                        v.tensor_copy(psm[:, g % 2, :, :].rearrange("p t (j k) -> p t j k", j=G)[:, :, :, 0:SB],
                                      pg[:, g % 2, :, :, RB:KA]).then_inc(s["small_in"], 1)
                    if not on_act(s, h):
                        more = None
                        if s["kind"] == "a" and h % G == G - 1:
                            more = lambda half: copy_small(b, h // G, half)
                        elif s["kind"] == "a" and h in WO_SLOTS and not first:
                            more = lambda half: guard_nan(b - 1, WO_SLOTS.index(h), half)
                        copy_probs(dve, s, b, h, n, G, more)
                    if s["kind"] == "a" and h in GUARD_SLOTS and not first:
                        guard_inf(b - 1, GUARD_SLOTS.index(h))
                    if s["kind"] != "b":
                        late_group(b, h, DIVIDE_SLOT, first, lambda bb, g: divide(s, bb, g))

            def copy_small(b, g, half):
                dve.wait_ge(*at(sa, "o_ps", b, g - 1))
                v.tensor_copy(psmT[:, g % 2, :], half)

            def guard_nan(b, t, half):
                dve.wait_ge(*at(sa, "wo_ps", b, t + 1))
                dve.wait_ge(*at(sa, "x_done", b, 0))
                part = slice(t * D, (t + 1) * D)
                link(sa, "guarded", b, 2 * t + 1, v.tensor_scalar(guard_t[:, part], half, 0.0, None, ALU.max))
                v.scalar_tensor_tensor(guard_z[:, part], half, 0.0, guard_t[:, part],
                                       op0=ALU.min, op1=ALU.add).then_inc(sa["guarded"], 1)

            def guard_inf(b, i):
                m = inf_m.bitcast(i32)
                wait_apart(dve, *at(sa, "guarded", b, 4 + i))
                if i % 2 == 0:
                    ins = v.tensor_scalar(m, guard_z, (FLT_MAX, -FLT_MAX)[i // 2], None,
                                          (ALU.is_gt, ALU.is_lt)[i // 2])
                else:
                    ins = v.copy_predicated(guard_z, m, (big_pos, big_neg)[i // 2][:, :].to_broadcast([P, NT * D]))
                ins.then_inc(sa["guarded"], 1)

            def divide(s, b, g):
                if g == 0 and s["kind"] == "a":
                    dve.wait_ge(*at(s, "yT_ps", b, 0))
                elif g == 0:
                    dve.wait_ge(*at(s, "x_done", b, 0))
                dve_divide(s, b, g)

            def start(s, step):
                for h in range(H):
                    step(0, 0, h)
                for h in range(lead(s["kind"])):
                    maxima(s, 0, h)

            def step_a(b, par, h):
                if h == 0:
                    dve_stats(sa, b)
                    dve_normalize(sa, b)
                elif h == 1:
                    dve.wait_ge(*at(sa, "xT", b, 1))
                    dve.wait_ge(*at(sa, "x_lo", b, 0))
                    link(sa, "hT", b, 1, v.tensor_scalar(guard_t, ps_a[:, :], 0.0, BIG, ALU.max, ALU.min))
                    link(sa, "hT", b, 2,
                         v.scalar_tensor_tensor(hT[:, :, 0:T], halves(ps_a), 0.0,
                                                guard_t.rearrange("p (c t) -> p c t", c=NC), op0=ALU.min, op1=ALU.add))
                    v.tensor_copy(hT[:, :, T:TX], hT[:, :, 0:TX - T]).then_inc(sa["hT"], 1)
                elif h in (5, 6, 7, 8):
                    n, n_t = ("k", KA_PAD) if h < 7 else ("q", T)
                    second = h % 2 == 0
                    r, bank = ((krot1, krot2) if h < 7 else (rot1, rot2))[second], (ps_a, ps_b)[second]
                    table = ((C_COSK, C_SINK) if h < 7 else (C_COS, C_SIN))[second]
                    dve.wait_ge(*at(sa, n + ("_ps", "r_ps")[second], b, 1))
                    dve.wait_ge(*at(sa, n + "_f", b, 0))
                    v.tensor_tensor(r, halves(bank)[:, :, 0:n_t],
                                    cst[:, table:table + n_t].unsqueeze(1).to_broadcast([P, NC, n_t]),
                                    ALU.mult).then_inc(sa[n + ("_rot1", "_rot2")[second]], 1)
                elif h == 9:
                    dve.wait_ge(*at(sa, "q_f", b, 1))
                    dve.wait_ge(*at(sa, "e_ps", b, 0))
                    for c in range(NC):
                        v.tensor_scalar(q_bd[:, c, :], cst[:, C_HM + c * H:C_HM + (c + 1) * H],
                                        q_f[:, c, T - 1:T], None, ALU.mult).then_inc(sa["q_last"], 1)
                    dve.wait_ge(*at(sa, "v_ps", b, 0))
                    dve.wait_ge(*at(sa, "x_lo", b, 1))
                    v.tensor_copy(rep_lo[:, :, :].rearrange("p c (g k) -> p c g k", g=G),
                                  x_lo[:, :, 0:VC].bitcast(f32).unsqueeze(2).to_broadcast([P, NC, G, VC])
                                  ).then_inc(sa["rep"], 1)
                elif h == 11:
                    dve.wait_ge(*at(sa, "e_ps", b, 1))
                    v.tensor_scalar(e_row[0:H, 0:KA], ps_b[0:H, 0:KA], FLT_MAX, FLT_MAX, ALU.min, ALU.min,
                                    accum_out=e_s[0:H, 2:3]).then_inc(sa["e_dve"], 1)
                elif h in (12, 13):
                    e = [e_s[0:H, i:i + 1] for i in range(16)]
                    step_n = lambda n, ins: link(sa, "e_dve", b, n, ins)
                    if h == 12:
                        dve.wait_ge(*at(sa, "e_exp", b, 3))
                        step_n(2, v.scalar_tensor_tensor(e[6], e[3], e[4], e[5], op0=ALU.add, op1=ALU.add))
                        step_n(3, v.reciprocal(e[7], e[6]))
                        step_n(4, v.tensor_tensor(e[8], e[3], e[7], ALU.mult))
                        step_n(5, v.tensor_tensor(e[9], e[4], e[7], ALU.mult))
                        v.tensor_scalar(e[10], e[9], 1.0 / (T - E_TOK - 1), 1e-6, ALU.mult, ALU.add)\
                            .then_inc(sa["e_dve"], 1)
                    else:
                        dve.wait_ge(*at(sa, "e_dve", b, 6))
                        step_n(7, v.reciprocal(e[11], e[10]))
                        step_n(8, v.tensor_tensor(e[12], e[8], e[11], ALU.mult))
                        step_n(9, v.tensor_scalar(e[13], e[12], 0.0, 1.0, ALU.max, ALU.min))
                        step_n(10, v.tensor_tensor(e[14], cst16[:, D + P:D + P + 1], e[13], ALU.is_lt))
                        v.scalar_tensor_tensor(b_row[0:H, :], ps_b[0:H, T:2 * T], e[14], cst16[:, 0:D],
                                               op0=ALU.mult, op1=ALU.mult).then_inc(sa["e_dve"], 1)
                elif h == 15:
                    dve.wait_ge(*at(sa, "v_big", b, 1))
                    for j in range(G):
                        rows = slice(j * VC, (j + 1) * VC)
                        last = v.tensor_copy(v_blk[par][rows, :, j, 0:HD],
                                             ps_a[rows, 0:D].rearrange("p (g j d) -> p g j d", g=G, j=G)[:, :, j, :])
                    last.then_inc(sa["v_small"], 1)

            def batch_a(b, par, first, last):
                heads(sa, b, par, first, last, T, step_a)

            dve.wait_ge(s_x, 16 * B)
            run_batches(dve, lambda: start(sa, step_a), batch_a)
            divide(sa, B - 1, H // G - 1)
            for t in range(NT):
                guard_nan(B - 1, t, ps_t[t][:, T:2 * T])
            for i in range(4):
                guard_inf(B - 1, i)
            dve.wait_ge(*at(sa, "x_done", B - 1, 1))

            def ffn(s, i):
                def step(b, par, h):
                    gate = lambda n, ins: link(s, "gate", b, n, ins)
                    if h == 0:
                        dve_stats(s, b)
                    elif h == 1:
                        dve_normalize(s, b)
                    elif h == 3:
                        dve_x_lo(s, b)
                    elif h == 5:
                        dve.wait_ge(*at(s, "gate_ps", b, 1))
                        gate(1, v.tensor_copy(lg, ps_a[:, 0:NT * H].rearrange("p (t h) -> p t h", t=NT)))
                        gate(2, v.tensor_reduce(g_s[:, :, 0], lg, AX.X, ALU.max))
                        top = g_s[:, :, 0:1].to_broadcast([P, NT, H])
                        v.tensor_tensor(g_d, lg, top, ALU.subtract).then_inc(s["gate"], 1)
                        v.tensor_tensor(g_eq, lg, top, ALU.is_equal).then_inc(s["gate"], 1)
                    elif h == 6:
                        dve.wait_ge(*at(s, "gate", b, 4))
                        gate(5, v.tensor_tensor(g_eq, g_eq, cst[:, C_DESC:C_DESC + H].unsqueeze(1)
                                                .to_broadcast([P, NT, H]), ALU.mult))
                        v.tensor_reduce(g_s[:, :, 1], g_eq, AX.X, ALU.max).then_inc(s["gate"], 1)
                        dve.wait_ge(*at(s, "q_hi", b, 1))
                        dve.wait_ge(q_put[i + 1], b * 32)
                        v.tensor_tensor(q_lo[:, :, :], halves(ps_b), q_hi[:, :, :].bitcast(f32),
                                        ALU.subtract).then_inc(s["q_lo"], 1)
                    elif h == 7:
                        dve.wait_ge(*at(s, "gate", b, 6))
                        gate(7, v.tensor_tensor(g_hot, g_eq, g_s[:, :, 1:2].to_broadcast([P, NT, H]), ALU.is_equal))
                        dve.wait_ge(*at(s, "k_ps", b, 1))
                        v.tensor_tensor(g_pick.rearrange("p t (h d) -> p t h d", h=H),
                                        halves(ps_a).rearrange("p t (h d) -> p t h d", h=H),
                                        g_hot.unsqueeze(3).to_broadcast([P, NT, H, HD]), ALU.mult).then_inc(s["k_sel"], 1)
                    elif h == 8:
                        dve.wait_ge(*at(s, "k_sel", b, 1))
                        v.tensor_reduce(kv_sh, g_pick.rearrange("p t (h d) -> p t d h", h=H), AX.X,
                                        ALU.add).then_inc(s["k_sel"], 1)
                    elif h == 9:
                        scale = HD ** -0.5
                        dve.wait_ge(*at(s, "k_sel", b, 2))
                        dve.wait_ge(*at(s, "kT_ps", b, 0))
                        link(s, "k48", b, 1, v.tensor_scalar(k48[:, :, 0:HD], kv_sh, scale, None, ALU.mult))
                        v.scalar_tensor_tensor(k48[:, :, HD:2 * HD], kv_sh, scale, k48[:, :, 0:HD].bitcast(f32),
                                               op0=ALU.mult, op1=ALU.subtract).then_inc(s["k48"], 1)
                        v.tensor_copy(k48[:, :, 2 * HD:3 * HD], k48[:, :, 0:HD].bitcast(f32)).then_inc(s["k48"], 1)
                        dve.wait_ge(*at(s, "gate_exp", b, 1))
                        v.tensor_reduce(g_s[:, :, 2], g_e, AX.X, ALU.add).then_inc(s["gate"], 1)
                    elif h == 10:
                        dve.wait_ge(*at(s, "gate", b, 8))
                        gate(9, v.reciprocal(g_s[:, :, 3], g_s[:, :, 2]))
                        v.tensor_tensor(g_hotv, g_hot, g_s[:, :, 3:4].to_broadcast([P, NT, H]), ALU.mult)\
                            .then_inc(s["gate"], 1)
                    elif h == 12:
                        dve.wait_ge(*at(s, "gate", b, 10))
                        dve.wait_ge(*at(s, "v_ps", b, 1))
                        v.tensor_tensor(g_pick.rearrange("p t (h d) -> p t h d", h=H),
                                        halves(ps_a).rearrange("p t (h d) -> p t h d", h=H),
                                        g_hotv.unsqueeze(3).to_broadcast([P, NT, H, HD]), ALU.mult)\
                            .then_inc(s["v_sel"], 1)
                    elif h == 13:
                        dve.wait_ge(*at(s, "v_sel", b, 1))
                        v.tensor_reduce(v_sh[par][:, :, 0:HD], g_pick.rearrange("p t (h d) -> p t d h", h=H), AX.X,
                                        ALU.add).then_inc(s["v_sel"], 1)

                run_batches(dve, lambda: start(s, step),
                            lambda b, par, first, last: heads(s, b, par, first, last, 3 * P, step))
                divide(s, B - 1, H // G - 1)
                dve.wait_ge(*at(s, "x_done", B - 1, 1))

            ffn(sf[0], 0)

            dve.wait_ge(s_stage, 16 * 6)
            dve.wait_ge(b_hi, 2)
            v.tensor_tensor(wb_lo[:, :, 0:W_ABS], st_pe[:, :, 0:W_ABS], wb_hi[:, :, 0:W_ABS].bitcast(f32),
                            ALU.subtract).then_inc(b_lo, 1)
            v.tensor_tensor(wb_lo[:, :, W_PE:W_COLS], st_pe[:, :, W_ABS:], wb_hi[:, :, W_PE:W_COLS].bitcast(f32),
                            ALU.subtract).then_inc(b_lo, 1)
            for i in range(4):
                dve.wait_ge(b_hi, i + 3)
                part = slice(W_ABS + (i % 2) * 512, W_ABS + (i % 2 + 1) * 512)
                v.tensor_tensor(wb_lo[:, i // 2, part], ps[i][:, :], wb_hi[:, i // 2, part].bitcast(f32),
                                ALU.subtract).then_inc(b_lo, 1)
            for i in range(4):
                dve.wait_ge(b_prep, i + 5)
                v.tensor_copy(m_vo[:, 2 * i:2 * i + 2, :], halves(ps[4 + i])).then_inc(b_mvo, 1)

            def rotary(dst, src, cos, sin, heads_dim):
                hr = ROPE // 2
                shape = [P, heads_dim, ROPE]
                tab = lambda c: c if c.shape[1] == heads_dim and len(c.shape) == 3 else \
                    c.unsqueeze(1).to_broadcast(shape)
                cos, sin = tab(cos), tab(sin)
                v.tensor_tensor(dst[0], src, cos, ALU.mult)
                v.tensor_tensor(dst[1][:, :, 0:hr], src[:, :, hr:ROPE], sin[:, :, 0:hr], ALU.mult)
                return v.tensor_tensor(dst[1][:, :, hr:ROPE], src[:, :, 0:hr], sin[:, :, hr:ROPE], ALU.mult)

            cosb = cst[:, C_COSB:C_COSB + NT * ROPE].rearrange("p (t d) -> p t d", t=NT)
            sinb = cst[:, C_SINB:C_SINB + NT * ROPE].rearrange("p (t d) -> p t d", t=NT)

            def step_b(b, par, h):
                if h == 0:
                    dve_stats(sm, b)
                elif h == 1:
                    dve_normalize(sm, b)
                elif h == 2:
                    dve_x_lo(sm, b)
                elif h == 3:
                    dve.wait_ge(*at(sm, "kva_ps", b, 1))
                    link(sm, "kva", b, 1, v.tensor_copy(kva_tok[:, :, :], halves(ps_b)[:, :, 0:W_ABS]))
                    for t in range(NT):
                        lat = kva_tok[:, t, 0:LORA]
                        v.tensor_tensor_reduce(out=k_rot[:, 0, t, :], in0=lat, in1=lat, scale=1.0, scalar=0.0,
                                               op0=ALU.mult, op1=ALU.add,
                                               accum_out=sq_sum[:, t:t + 1]).then_inc(sm["kva"], 1)
                elif h == 5:
                    dve.wait_ge(*at(sm, "kva", b, 3))
                    link(sm, "k_tok", b, 1, rotary((k_rot[:, 0], k_rot[:, 1]), kva_tok[:, :, LORA:W_ABS],
                                                   cosb, sinb, NT))
                    v.tensor_tensor(kv_tok[par][:, :, LORA:W_ABS], k_rot[:, 0], k_rot[:, 1], ALU.add)
                    dve.wait_ge(*at(sm, "rms", b, 2))
                    for t in range(NT):
                        last = v.scalar_tensor_tensor(kv_tok[par][:, t, 0:LORA], kva_tok[:, t, 0:LORA],
                                                      rms[:, t:t + 1], norm_bc[:, :], op0=ALU.mult, op1=ALU.mult)
                    last.then_inc(sm["k_tok"], 1)
                for i in Q_SLOTS.get(h, ()):
                    if i % 2 == 1:
                        dve.wait_ge(*at(sm, "qr_ps", b, i // 2 + 1))
                        dve.wait_ge(*at(sm, "qr_out", b, i // 2))
                        rotary([r[:, :, :].rearrange("p c (e d) -> p (c e) d", d=ROPE) for r in (rope1, rope2)],
                               ps_b[:, :].rearrange("p (h d) -> p h d", h=8), cosb[:, i // 4, :], sinb[:, i // 4, :],
                               8).then_inc(sm["qr_dve"], 1)
                for i in QT_SLOTS.get(h, ()):
                    if i % 2 == 1:
                        dve.wait_ge(*at(sm, "qT_ps", b, i + 1))
                        v.tensor_copy(qT[par][:, 2 * i:2 * i + 2, :], halves(ps_a)).then_inc(sm["qT_dve"], 1)

            def batch_b(b, par, first, last):
                heads(sm, b, par, first, last, 3 * P, step_b)
                dve.wait_ge(*at(sm, "wo_ps", b, H // 2))
                v.tensor_tensor(x_batch(b), ps_s[2][:, :], x_batch(b), ALU.add).then_inc(sm["x_done"], 1)

            run_batches(dve, lambda: start(sm, step_b), batch_b)
            dve.wait_ge(*at(sm, "x_done", B - 1, 1))
            ffn(sf[1], 1)

        @blk.tensor
        def _(pe):
            mm, transpose = nc.tensor.matmul, nc.tensor.transpose
            pe.wait_ge(s_split, 4)
            pe.wait_ge(s_fill, N_FILLS)
            pe.wait_ge(s_dfill, N_DVE_FILLS)
            pe.wait_ge(s_arena, N_ARENA)
            pe.wait_ge(s_w, 64)

            def mask(out_ap, stop=True):
                return mm(out_ap, ident_bf[:, :], mask_bf[:, :], start=False, stop=True, skip_group_check=True)

            def scores(s, b, par, h, i=0):
                if s["kind"] == "a":
                    if h == 0:
                        pe.wait_ge(q_got[0], b * 48 + 48)
                        pe.wait_ge(k_got, b * 48 + 48)
                    pe.wait_ge(*at(s, "maxed", b, before(h)))
                    for t in range(NT):
                        last = mm(halves(ps_s[slot_of(h)])[:, t, 0:KA_PAD], q_stack[par][:, h, t * P:(t + 1) * P],
                                  ka_stack[par][:, h, :], start=True, stop=True)
                elif s["kind"] == "f":
                    if h == 0:
                        pe.wait_ge(q_got[i + 1], b * 48 + 48)
                        pe.wait_ge(*at(s, "k_stack", b, 1))
                    pe.wait_ge(*at(s, "exp", b, before(h)))
                    for t in range(NT):
                        o = halves(ps_s[slot_of(h)])[:, t, :]
                        mm(o, q_stack[par][:, h, t * P:(t + 1) * P], kf_stack[par][:, :], start=True, stop=True)
                        last = mask(o[:, t * P:(t + 1) * P])
                else:
                    if h == 0:
                        pe.wait_ge(*at(s, "kT", b, 1))
                    if h % 2 == 0:
                        pe.wait_ge(*at(s, "qT_dve" if h // 2 % 2 else "qT_act", b, h // 4 + 1))
                    pe.wait_ge(*at(s, "exp", b, h - 1))
                    for t in range(NT):
                        o = ps_s[h % 2][:, t * P:t * P + (t + 1) * P]
                        mm(o, qT[par][:, h, t * P:(t + 1) * P], kbT[par][:, 0:(t + 1) * P], start=True, stop=True)
                        last = mask(o[:, t * P:(t + 1) * P])
                last.then_inc(s["scores"], 1)

            def heads(s, b, par, first, last, step, i=0):
                for h in range(H):
                    ahead = h + lead(s["kind"]) + 1
                    if ahead < H:
                        scores(s, b, par, ahead, i)
                    elif not last:
                        scores(s, b + 1, 1 - par, ahead - H, i)
                    if not last:
                        step(b + 1, 1 - par, h)
                    if s["kind"] == "a":
                        pe.wait_ge(*at(s, "exp", b, h + 1))
                        more = None
                        if h % G == G - 1:
                            more = lambda half: small_transposes(b, h // G, half)
                        elif h in YT_SLOTS and not first:
                            more = lambda half: transpose_y(b - 1, YT_SLOTS.index(h), half)
                        elif h in WO_SLOTS and not first:
                            more = lambda half: project_y(b - 1, WO_SLOTS.index(h), half)
                        pe_transpose_probs(s, b, h, [pg[:, h // G % 2, t, h % G, 0:P] for t in range(NT)], more)
                        late_group(b, h, PV_SLOT, first,
                                   lambda bb, g: outputs_a(bb, par if g * G + PV_SLOT < H else 1 - par, g))
                    elif s["kind"] == "f":
                        pe.wait_ge(*at(s, "exp", b, h + 1))
                        pe_transpose_probs(s, b, h, [probs[:, h % 4, k * P:(k + 1) * P] for k in range(3)])
                        late_group(b, h, PV_SLOT, first,
                                   lambda bb, g: outputs_f(s, bb, par if g * G + PV_SLOT < H else 1 - par, g))
                    else:
                        pe.wait_ge(*at(s, "normed", b, 2 * h + 2))
                        pe_transpose_probs(s, b, h, [probs[:, h % 4, k * P:(k + 1) * P] for k in range(3)])
                        if h % 2 == 0 and h:
                            attend_b(b, par, h // 2 - 1)
                        if h % 2 == 1 and h > 2:
                            project_b(b, (h - 3) // 2)
                    if s["kind"] != "b":
                        late_group(b, h, BACK_SLOT, first, lambda bb, g: pe_untranspose(s, bb, g))

            def small_transposes(b, g, half):
                pe.wait_ge(*at(sa, "small_in", b, g + 1))
                for t in range(NT):
                    transpose(half[:, t * P:(t + 1) * P], psm[:, g % 2, t, :], ident)

            def transpose_y(b, c, half):
                pe.wait_ge(*at(sa, "y", b, 3 * H // G))
                for t in range(NT):
                    last = transpose(half[:, t * P:(t + 1) * P], y[:, t, c * P:(c + 1) * P], ident)
                last.then_inc(sa["yT_ps"], 1)

            def project_y(b, t, half):
                pe.wait_ge(*at(sa, "yT", b, NC))
                for c in range(NC):
                    last = mm(half, yT[:, c, t * P:(t + 1) * P], wo_a[:, c, :], start=c == 0, stop=c == NC - 1)
                last.then_inc(sa["wo_ps"], 1)

            def outputs_a(b, par, g):
                pe_wait_copies(sa, b, g * G, G)
                pe.wait_ge(*at(sa, "y", b, 3 * g))
                if g == 0:
                    pe.wait_ge(*at(sa, "v_big", b, 1))
                    pe.wait_ge(*at(sa, "v_small", b, 1))
                mm(ps_o[:, 0:T], v_blk[par][:, g, :, :].rearrange("p j c -> p (j c)"), psmT[:, g % 2, :], start=True, stop=False,
                   skip_group_check=True)
                for j in range(G):
                    h = g * G + j
                    last = mm(ps_o[j * VC:(j + 1) * VC, 0:T], v_big[par][:, h, :], probsT[:, h % 8, 0:T],
                              start=False, stop=True, skip_group_check=True)
                last.then_inc(sa["o_ps"], 1)

            def outputs_f(s, b, par, g):
                pe_wait_copies(s, b, g * G, G)
                pe.wait_ge(*at(s, "y", b, 3 * g))
                if g == 0:
                    pe.wait_ge(*at(s, "v_sel", b, 2))
                for k, (lo, n) in enumerate(((0, T), (T, P))):
                    for j in range(G):
                        last = mm(ps_o[j * VC:(j + 1) * VC, T - n:T], v_sh[par][:, k, :],
                                  probsT[:, (g * G + j) % 8, lo:lo + n], start=k == 0, stop=k == 1,
                                  skip_group_check=True)
                last.then_inc(s["o_ps"], 1)

            def start(s, step, i=0):
                for h in range(H):
                    step(0, 0, h)
                for h in range(lead(s["kind"]) + 1):
                    scores(s, 0, 0, h, i)

            def step_a(b, par, h):
                if h == 1:
                    pe.wait_ge(*at(sa, "v_big", b, 0))
                    pe.wait_ge(*at(sa, "v_small", b, 0))
                    pe_transpose_x(sa, b)
                elif h in (4, 5, 6, 7):
                    n = ("k_ps", "kr_ps", "q_ps", "qr_ps")[h - 4]
                    if h == 4:
                        pe.wait_ge(*at(sa, "x_lo", b, 1))
                    elif h == 5:
                        pe.wait_ge(*at(sa, "e_dve", b, 0))
                    else:
                        pe.wait_ge(*at(sa, ("k_rot1", "k_rot2")[h - 6], b, 1))
                    bank, w = (ps_a, ps_b)[h % 2], (2, 3, 0, 1)[h - 4]
                    lo, n_t = (T - RB, KA_PAD) if h < 6 else (0, T)
                    for c in range(NC):
                        last = mm3(halves(bank)[:, c, 0:n_t], cols(AW, w * D + c * P, P), cols(X, lo, n_t))
                    last.then_inc(sa[n], 1)
                elif h == 10:
                    pe.wait_ge(*at(sa, "k_f", b, 1))
                    pe.wait_ge(*at(sa, "q_last", b, 2))
                    for c in range(NC):
                        mm(ps_b[0:H, 0:KA_PAD], q_bd[:, c, :], k_f[:, c, :], start=c == 0, stop=c == NC - 1)
                    tok = tuple((lambda c, w=w: w[:, c, E_TOK:E_TOK + 1].to_broadcast([P, P])) for w in X)
                    mm3(ps_b[:, T:2 * T], tok, cols(AW, 4 * D, D)).then_inc(sa["e_ps"], 1)
                elif h == 14:
                    pe.wait_ge(*at(sa, "q_rot1", b, 1))
                    pe.wait_ge(*at(sa, "e_dve", b, 11))
                    pe.wait_ge(*at(sa, "rep", b, 2))
                    mm3(ps_a[:, 0:D], cols((rep_hi, rep_lo), 0, P), cols(AW, 4 * D, D))
                    mm3(ps_a[:, D:2 * D], cols(X, P, P), cols(AW, 4 * D, D), stop=False)
                    mm(ps_a[:, D:2 * D], cst16[:, D:D + P], b_row[0:H, :], start=False, stop=True)\
                        .then_inc(sa["v_ps"], 1)

            def batch_a(b, par, first, last):
                heads(sa, b, par, first, last, step_a)

            run_batches(pe, lambda: start(sa, step_a), batch_a)
            outputs_a(B - 1, 1, H // G - 1)
            pe_untranspose(sa, B - 1, H // G - 1)
            for act in (True, False):
                pe.wait_ge(*copied(sa, B - 1, H - 1, act))
            for c in range(NC):
                transpose_y(B - 1, c, ps_t[c][:, T:2 * T])
            for t in range(NT):
                project_y(B - 1, t, ps_t[t][:, T:2 * T])
            pe.wait_ge(*at(sa, "x_done", B - 1, 1))

            def ffn(s, i):
                def step(b, par, h):
                    if h == 2:
                        pe.wait_ge(*at(s, "v_sel", b, 0))
                        pe_transpose_x(s, b)
                    elif h == 4:
                        pe.wait_ge(*at(s, "x_lo", b, 1))
                        for t in range(NT):
                            last = mm3(ps_a[:, t * H:(t + 1) * H], cols(X, t * P, P), cols(FW, F_G, H))
                        last.then_inc(s["gate_ps"], 1)
                        pe.wait_ge(*at(s, "k_stack", b, 0))
                        mm3(halves(ps_b)[:, 0, :], cols(FW, 0, P), cols(X, 0, T))
                    elif h == 5:
                        mm3(halves(ps_b)[:, 1, :], cols(FW, P, P), cols(X, 0, T)).then_inc(s["q_ps"], 1)
                    elif h == 6:
                        pe.wait_ge(*at(s, "gate", b, 1))
                        for t in range(NT):
                            last = mm3(halves(ps_a)[:, t, :], cols(X, t * P, P), cols(FW, F_K, D))
                        last.then_inc(s["k_ps"], 1)
                    elif h == 9:
                        pe.wait_ge(*at(s, "k_sel", b, 1))
                        for t in range(NT):
                            last = mm3(halves(ps_a)[:, t, :], cols(X, t * P, P), cols(FW, F_V, D))
                        last.then_inc(s["v_ps"], 1)
                    elif h == 10:
                        pe.wait_ge(*at(s, "q_lo", b, 1))
                        wait_apart(pe, *at(s, "k48", b, 3))
                        for t in range(NT):
                            last = transpose(ps_b[0:3 * HD, t * P:(t + 1) * P], k48[:, t, :].bitcast(f32), ident)
                        last.then_inc(s["kT_ps"], 1)

                run_batches(pe, lambda: start(s, step, i),
                            lambda b, par, first, last: heads(s, b, par, first, last, step, i))
                outputs_f(s, B - 1, 1, H // G - 1)
                pe_untranspose(s, B - 1, H // G - 1)
                pe.wait_ge(*at(s, "x_done", B - 1, 1))

            ffn(sf[0], 0)

            pe.wait_ge(s_stage, 16 * 6)
            for i in range(4):
                for k in range(8):
                    h = (i % 2) * 8 + k
                    last = mm(ps[i][:, k * LORA:(k + 1) * LORA], st_wqn[:, h, (i // 2) * P:(i // 2 + 1) * P],
                              st_wk[:, h, :], start=True, stop=True)
                last.then_inc(b_prep, 1)
            for i in range(4):
                for r in range(2):
                    for j in range(2):
                        h = (2 * i + r) * 2 + j
                        last = mm(ps[4 + i][j * LORA:(j + 1) * LORA, r * D:(r + 1) * D], st_wv[:, h, :],
                                  st_wo[:, h, :], start=True, stop=True)
                last.then_inc(b_prep, 1)
            pe.wait_ge(b_lo, 6)
            pe.wait_ge(b_mvo, 4)

            def attend_b(b, par, p):
                pe_wait_copies(sm, b, 2 * p, 2)
                pe.wait_ge(*at(sm, "oT", b, p))
                for k, (lo, n) in enumerate(((0, T), (T, P))):
                    for j in range(2):
                        last = mm(halves(ps_o)[j * LORA:(j + 1) * LORA, p % 2, T - n:T], kv_tok[par][:, k, 0:LORA],
                                  probsT[:, (2 * p + j) % 8, lo:lo + n], start=k == 0, stop=k == 1,
                                  skip_group_check=True)
                last.then_inc(sm["o_ps"], 1)

            def project_b(b, p):
                pe.wait_ge(*at(sm, "oT", b, p + 1))
                if p == 0:
                    pe.wait_ge(*at(sm, "x_done", b, 0))
                for t in range(NT):
                    last = mm(halves(ps_s[2])[:, t, :], oT[:, p % 2, t * P:(t + 1) * P], m_vo[:, p, :],
                              start=p == 0 and t == 0, stop=p == H // 2 - 1, skip_group_check=True)
                last.then_inc(sm["wo_ps"], 1)

            def step_b(b, par, h):
                if h == 1:
                    pe.wait_ge(*at(sm, "qT_dve", b, 0))
                    pe_transpose_x(sm, b)
                elif h == 3:
                    pe.wait_ge(*at(sm, "x_lo", b, 1))
                    pe.wait_ge(*at(sm, "qT_act", b, 0))
                    for t in range(NT):
                        last = mm3(halves(ps_b)[:, t, 0:192], cols(X, t * P, P), cols(WB, 0, 192))
                    last.then_inc(sm["kva_ps"], 1)
                for i in Q_SLOTS.get(h, ()):
                    t, hh, rot = i // 4, i // 2 % 2, i % 2
                    if rot:
                        pe.wait_ge(*at(sm, "kva", b, 1))
                        pe.wait_ge(*at(sm, "qr_dve", b, i // 2))
                    else:
                        pe.wait_ge(*at(sm, "qa_out", b, i // 2))
                    mm3((ps_a, ps_b)[rot][:, :], cols(X, t * P, P), cols(WB, (W_ABS, W_PE)[rot] + hh * 512, 512))\
                        .then_inc((sm["qa_ps"], sm["qr_ps"])[rot], 1)
                if h == 9:
                    pe.wait_ge(*at(sm, "qa_out", b, 4))
                    pe.wait_ge(*at(sm, "k_tok", b, 2))
                    for t in range(NT):
                        last = transpose(ps_a[:, t * P:(t + 1) * P], kv_tok[par][:, t, :], ident)
                    last.then_inc(sm["kT_ps"], 1)
                for i in QT_SLOTS.get(h, ()):
                    pe.wait_ge(*at(sm, "qr_out", b, 4))
                    if i % 2:
                        pe.wait_ge(*at(sm, "kT", b, 1))
                        pe.wait_ge(*at(sm, "qT_dve", b, i // 2))
                    else:
                        pe.wait_ge(*at(sm, "qr_dve", b, 4))
                        pe.wait_ge(*at(sm, "qT_act", b, i // 2))
                    for j in range(2):
                        for t in range(NT):
                            last = transpose(halves((ps_b, ps_a)[i % 2])[:, j, t * P:(t + 1) * P],
                                             q_tok[:, t, 2 * i + j, :], ident)
                    last.then_inc(sm["qT_ps"], 1)

            def batch_b(b, par, first, last):
                heads(sm, b, par, first, last, step_b)
                attend_b(b, par, H // 2 - 1)
                project_b(b, H // 2 - 1)

            run_batches(pe, lambda: start(sm, step_b), batch_b)
            pe.wait_ge(*at(sm, "x_done", B - 1, 1))
            ffn(sf[1], 1)


def constants():
    import numpy as np

    f = np.float32
    c = np.zeros((P, C_END), f)
    c[:, C_ID:C_ID + P] = np.eye(P, dtype=f)
    c[:, C_MASK:C_MASK + P] = np.where(np.arange(P)[None, :] > np.arange(P)[:, None], f(-1e30), f(0))
    pos = np.arange(T, dtype=f)
    inv = (f(1.0) / f(10000.0) ** (np.arange(0, HD, 2, dtype=f) / f(HD))).astype(f)
    ang = pos[None, :] * inv[:, None]
    ang = np.tile(np.concatenate([ang, ang]), (P // HD, 1)).astype(f)
    sign = np.tile(np.repeat(np.array([-1, 1], f), HD // 2), P // HD)[:, None]
    k_scale = f(-(HD ** -0.5))
    keys = np.concatenate([np.arange(T - RB, T), np.arange(KA_PAD - RB)])
    for lo, table in ((C_COS, np.cos(ang)), (C_SIN, np.sin(ang) * sign),
                      (C_COSK, np.cos(ang[:, keys]) * k_scale), (C_SINK, np.sin(ang[:, keys]) * sign * k_scale)):
        c[:, lo:lo + table.shape[1]] = table
    for t in range(NC):
        for p in range(P):
            c[p, C_HM + t * H + (t * P + p) // HD] = 1
    c[:, C_DESC:C_DESC + H] = H - np.arange(H, dtype=f)
    inv = (f(1.0) / f(10000.0) ** (np.arange(0, ROPE, 2, dtype=f) / f(ROPE))).astype(f)
    ang = (pos[:, None] * inv[None, :]).astype(f).reshape(NT, P, ROPE // 2).transpose(1, 0, 2)
    cos, sin = np.cos(ang), np.sin(ang)
    c[:, C_COSB:C_COSB + NT * ROPE] = np.concatenate([cos, cos], 2).reshape(P, -1)
    c[:, C_SINB:C_SINB + NT * ROPE] = np.concatenate([-sin, sin], 2).reshape(P, -1)
    c16 = np.zeros((H, D + P), f)
    for h in range(H):
        c16[h, h * HD:(h + 1) * HD] = 1
    c16[:, D + 1:] = f(1.0 / RB)
    return c, c16


def kernel(**inputs):
    import numpy as np
    import concourse.bacc as bacc
    from concourse import mybir
    from concourse.bass_utils import run_bass_kernel_spmd

    w = {k: np.asarray(v) for k, v in inputs.items()}
    turned = (np.arange(D) // HD) * HD + (np.arange(D) % HD + HD // 2) % HD
    wq, wk, wv = (w[f"L0_attn_a_w{n}"] for n in "qkv")
    qkv, gate = w["L0_ffn_W_qkv"], w["L0_ffn_W_gate"]
    bq = w["L0_attn_b_wq"].reshape(D, H, QH)
    bkv = w["L0_attn_b_wkv_b"].reshape(LORA, H, NOPE + VD)
    consts, consts16 = constants()
    arrays = {
        "x": w["L0_attn_a_hidden_states"],
        "a_wT": np.concatenate([wq, wq[turned], wk, wk[turned], wv]).T,
        "a_woT": w["L0_attn_a_wo"].T,
        "a_u": w["L0_attn_a_bern_u"].T,
        "f_wT": np.concatenate([qkv[0:D], qkv[2 * D:], qkv[D:2 * D], gate]).T,
        "b_wqn": bq[:, :, 0:NOPE].transpose(2, 1, 0),
        "b_wqp": bq[:, :, NOPE:].reshape(D, H * ROPE),
        "b_wkT": bkv[:, :, 0:NOPE].transpose(2, 1, 0),
        "b_wvT": bkv[:, :, NOPE:].transpose(2, 1, 0),
        "b_wo": w["L0_attn_b_wo"],
        "b_wkva": w["L0_attn_b_wkv_a"],
        "b_norm": w["L0_attn_b_kv_norm_scale"],
        "consts": consts,
        "consts16": consts16,
    }
    arrays = {k: np.ascontiguousarray(v) for k, v in arrays.items()}
    nc = bacc.Bacc("TRN2", target_bir_lowering=False, num_devices=1)
    args = [nc.dram_tensor(k, v.shape, mybir.dt.from_np(v.dtype), kind="ExternalInput").ap()
            for k, v in arrays.items()]
    out = nc.dram_tensor("out", (B, T, D), mybir.dt.float32, kind="ExternalOutput").ap()
    hybrid_layers_kernel(nc, *args, out)
    r = run_bass_kernel_spmd(nc, [arrays], core_ids=[0])
    return r.results[0]["out"]
```
